# Optimizing a Trainium2 kernel written in Bass

```python
import numpy as np
import jax
import jax.numpy as jnp

def _softmax(x, axis=-1):
    return jax.nn.softmax(x, axis=axis)

def _gelu(x):
    return jax.nn.gelu(x, approximate=True)

def _silu(x):
    return jax.nn.silu(x)

def _sigmoid(x):
    return jax.nn.sigmoid(x)

def _layernorm(x, axis=-1, eps=1e-05):
    m = jnp.mean(x, axis=axis, keepdims=True)
    v = jnp.var(x, axis=axis, keepdims=True)
    return (x - m) / jnp.sqrt(v + eps)

def _scatter_add(tgt, idx, src, axis=0):
    return tgt.at[idx].add(src)

def _segment_sum(src, seg, n):
    return jax.ops.segment_sum(src, seg, n)
kernel_name = 'mk_adj_preln_d2_adj_r2_7d0d3c'

def setup_inputs(seed: int=0):
    np.random.seed(seed)
    _w = jnp.asarray

    def _rec_inputs():
        import jax
        import jax.numpy as jnp
        _gk = jax.random.key(seed)
        x = 7.22e-05 + 1 * jax.random.normal(jax.random.fold_in(_gk, 1), (128, 128, 128), jnp.float32)
        _w = (1.0 + jnp.arange(128, dtype=jnp.float32)) ** (-0.5)
        _w = _w / _w.mean()
        _pij = jnp.clip(0.0625 * _w[:, None] * _w[None, :], 0.0, 1.0)
        _a = jax.random.uniform(jax.random.fold_in(_gk, 2), (128, 128, 128)) < _pij
        _af = _a.astype(jnp.float32)
        adj = _af
        _nm = jnp.ones((128, 128), dtype=bool)
        nodemask = jnp.where(_nm, 1.0, 0.0).astype(jnp.float32)
        return (x, adj, nodemask)
    x, adj, nodemask = _rec_inputs()

    def _L0_gnn_setup():
        import jax, jax.numpy as jnp
        import numpy as np
        B, N, D, C, L = (64, 256, 128, 128, 5)
        EDGE_P = 0.02

        def _gru_cell(m, h, w_ih, w_hh, b_ih, b_hh):
            gi = m @ w_ih.T + b_ih
            gh = h @ w_hh.T + b_hh
            i_r, i_z, i_n = jnp.split(gi, 3, axis=-1)
            h_r, h_z, h_n = jnp.split(gh, 3, axis=-1)
            r = jax.nn.sigmoid(i_r + h_r)
            z = jax.nn.sigmoid(i_z + h_z)
            n = jnp.tanh(i_n + r * h_n)
            return (1.0 - z) * n + z * h
        key = jax.random.key(seed)
        ks = jax.random.split(key, 8)
        x = jax.random.normal(ks[0], (B, N, D), dtype=jnp.float32)
        adj = (jax.random.uniform(ks[1], (B, N, N)) < EDGE_P).astype(jnp.float32)
        mask = jnp.ones((B, N), dtype=jnp.float32)
        s = 1.0 / np.sqrt(C).astype(np.float32)
        weight = jax.random.uniform(ks[2], (L, C, C), minval=-s, maxval=s, dtype=jnp.float32)
        w_ih = jax.random.uniform(ks[3], (3 * C, C), minval=-s, maxval=s, dtype=jnp.float32)
        w_hh = jax.random.uniform(ks[4], (3 * C, C), minval=-s, maxval=s, dtype=jnp.float32)
        b_ih = jax.random.uniform(ks[5], (3 * C,), minval=-s, maxval=s, dtype=jnp.float32)
        b_hh = jax.random.uniform(ks[6], (3 * C,), minval=-s, maxval=s, dtype=jnp.float32)
        return dict(x=x, adj=adj, mask=mask, weight=weight, w_ih=w_ih, w_hh=w_hh, b_ih=b_ih, b_hh=b_hh)
    _L0_gnn_all = _L0_gnn_setup()
    _L0_gnn_in = {k: v for k, v in _L0_gnn_all.items() if k in ('weight', 'w_ih', 'w_hh', 'b_ih', 'b_hh')}
    del _L0_gnn_all

    def _L1_gnn_setup():
        import jax, jax.numpy as jnp
        import numpy as np
        B, N, D, H = (8, 1024, 128, 512)
        RMS_EPS = 1e-06

        def _rmsnorm(h, w, eps=RMS_EPS):
            var = jnp.mean(jnp.square(h), axis=-1, keepdims=True)
            return h * jax.lax.rsqrt(var + eps) * w
        key = jax.random.key(seed)
        ks = jax.random.split(key, 5)
        x = jax.random.normal(ks[0], (B, N, D), dtype=jnp.float32)
        adjacency = jax.random.uniform(ks[1], (B, N, N), dtype=jnp.float32)
        epsilon = jnp.zeros((), dtype=jnp.float32)
        W1 = jax.random.normal(ks[2], (D, H), dtype=jnp.float32) * (1.0 / np.sqrt(D))
        b1 = jnp.zeros((H,), dtype=jnp.float32)
        rms_weight = jnp.ones((H,), dtype=jnp.float32)
        W2 = jax.random.normal(ks[3], (H, D), dtype=jnp.float32) * (1.0 / np.sqrt(H))
        b2 = jnp.zeros((D,), dtype=jnp.float32)
        return {'x': x, 'adjacency': adjacency, 'epsilon': epsilon, 'W1': W1, 'b1': b1, 'rms_weight': rms_weight, 'W2': W2, 'b2': b2}
    _L1_gnn_all = _L1_gnn_setup()
    _L1_gnn_in = {k: v for k, v in _L1_gnn_all.items() if k in ('epsilon', 'W1', 'b1', 'rms_weight', 'W2', 'b2')}
    del _L1_gnn_all
    return {'x': x, 'adj': adj, 'nodemask': nodemask, 'L0_gnn_weight': _L0_gnn_in['weight'], 'L0_gnn_w_ih': _L0_gnn_in['w_ih'], 'L0_gnn_w_hh': _L0_gnn_in['w_hh'], 'L0_gnn_b_ih': _L0_gnn_in['b_ih'], 'L0_gnn_b_hh': _L0_gnn_in['b_hh'], 'L1_gnn_epsilon': _L1_gnn_in['epsilon'], 'L1_gnn_W1': _L1_gnn_in['W1'], 'L1_gnn_b1': _L1_gnn_in['b1'], 'L1_gnn_rms_weight': _L1_gnn_in['rms_weight'], 'L1_gnn_W2': _L1_gnn_in['W2'], 'L1_gnn_b2': _L1_gnn_in['b2']}

def reference(x, adj, nodemask, L0_gnn_weight, L0_gnn_w_ih, L0_gnn_w_hh, L0_gnn_b_ih, L0_gnn_b_hh, L1_gnn_epsilon, L1_gnn_W1, L1_gnn_b1, L1_gnn_rms_weight, L1_gnn_W2, L1_gnn_b2):
    import jax
    import jax.numpy as jnp

    def _L0_gnn_ref(x, adj, mask, weight, w_ih, w_hh, b_ih, b_hh):
        import jax, jax.numpy as jnp
        import numpy as np
        B, N, D, C, L = (64, 256, 128, 128, 5)
        EDGE_P = 0.02

        def _gru_cell(m, h, w_ih, w_hh, b_ih, b_hh):
            gi = m @ w_ih.T + b_ih
            gh = h @ w_hh.T + b_hh
            i_r, i_z, i_n = jnp.split(gi, 3, axis=-1)
            h_r, h_z, h_n = jnp.split(gh, 3, axis=-1)
            r = jax.nn.sigmoid(i_r + h_r)
            z = jax.nn.sigmoid(i_z + h_z)
            n = jnp.tanh(i_n + r * h_n)
            return (1.0 - z) * n + z * h
        A = (adj != 0).astype(x.dtype)
        h = x
        for l in range(weight.shape[0]):
            m = jnp.einsum('bnd,de->bne', h, weight[l])
            agg = jnp.einsum('bij,bid->bjd', A, m)
            h = _gru_cell(agg, h, w_ih, w_hh, b_ih, b_hh)
        return h * mask[..., None]

    def _L1_gnn_ref(x, adjacency, epsilon, W1, b1, rms_weight, W2, b2):
        import jax, jax.numpy as jnp
        import numpy as np
        B, N, D, H = (8, 1024, 128, 512)
        RMS_EPS = 1e-06

        def _rmsnorm(h, w, eps=RMS_EPS):
            var = jnp.mean(jnp.square(h), axis=-1, keepdims=True)
            return h * jax.lax.rsqrt(var + eps) * w
        neighbor_sum = jnp.einsum('bnm,bmd->bnd', adjacency, x)
        agg = epsilon * x + neighbor_sum
        h = jnp.einsum('bnd,dh->bnh', agg, W1) + b1
        h = jax.nn.silu(_rmsnorm(h, rms_weight))
        out = jnp.einsum('bnh,hd->bnd', h, W2) + b2
        return out
    h = jnp.maximum(_layernorm(x, axis=-1), 0.0)
    x = x + _L0_gnn_ref(h, adj, nodemask, L0_gnn_weight, L0_gnn_w_ih, L0_gnn_w_hh, L0_gnn_b_ih, L0_gnn_b_hh)
    h = jnp.maximum(_layernorm(x, axis=-1), 0.0)
    x = x + _L1_gnn_ref(h, adj, L1_gnn_epsilon, L1_gnn_W1, L1_gnn_b1, L1_gnn_rms_weight, L1_gnn_W2, L1_gnn_b2)
    return x

_drawn_inputs = setup_inputs


def setup_inputs(seed=0):
    import zlib

    import numpy as np

    out = dict(_drawn_inputs(seed))
    spreads = {'L1_gnn_b1': (0.0, 0.1), 'L1_gnn_rms_weight': (1.0, 0.2), 'L1_gnn_b2': (0.0, 0.1)}
    factors = {}
    for name, (base, spread) in spreads.items():
        noise = np.random.default_rng([zlib.crc32(name.encode()), seed]).standard_normal(out[name].shape)
        drawn = base * np.exp(spread * noise) if base else spread * noise
        out[name] = jnp.asarray(drawn.astype(out[name].dtype))
    for name, factor in factors.items():
        out[name] = (out[name] * factor).astype(out[name].dtype)
    return out
```

```python
from contextlib import ExitStack

import concourse.bass as bass
from concourse import mybir

ALU = mybir.AluOpType
ACT = mybir.ActivationFunctionType
F32 = mybir.dt.float32
F16 = mybir.dt.float16

P = 128
HI, LO = 0, 1

STATE_SCALE = 2.0 ** 5
WEIGHT_SCALE = 2.0 ** 8
GATE_SCALE = STATE_SCALE * WEIGHT_SCALE
AGG_SCALE = 2.0 ** 3
GRAM_SCALE = 2.0 ** 6
ACTIVE_SCALE = 2.0 ** 5
LN_EPS = 1e-5
RMS_EPS = 1e-6

GRAPHS = 4
STREAMS = 2
STEP = 26

AT_LAYER = dict(
    turn_hi=3, hidden_r_hi=3, turn_lo=3, hidden_r_lo=4, agg_of_hi=6, agg_of_lo=6, hidden_n=6, input_r=9, input_n=12, gate_z=15,
    copy_hi=1, copy_lo=3, agg_hi=4, sigmoid_r=8, sigmoid_z=13, tanh=19, state_hi=23,
    agg_lo=4, reset=9, add_input=13, z_state=16, mix=19, new_state=19, edges=9,
    state_lo=21,
)
AT_TAIL = dict(
    back=0, sums=14, gram=17, mean_sq=19, rows=27,
    chunk0=26, chunk1=29, chunk2=33, chunk3=42,
    project0=49, project1=59, project2=61, project3=62, turn_adj=47, turn_state0=61,
    relu1=6, sums_hi=10, copy_rows=24, relu0=20,
    sigmoid0=29, sigmoid1=33, sigmoid2=42, sigmoid3=49, hi0=37, hi1=46, hi2=50, hi3=59,
    node_hi0=46,
    x1=1, stats1=1, shift1=4, sums_lo=9, gram_prod=13, mean_sq_read=17,
    norm0=25, norm1=29, norm2=36, norm3=41, silu0=31, silu1=40, silu2=46, silu3=53, out=63,
    stats0=8, shift0=15, node_lo0=53, copy_state0=61, add_epsilon=50,
    x1_b2=30, pow1=1, pow_ms=20, pow0=13, lo0=44, lo1=57, lo2=57, lo3=58, state0=62,
    load_adj=3, load_res=5, load_x=34, store=52,
)


def gnn_pair_kernel(nc, x, adj, nodemask, gru_weight, w_ih, w_hh, b_ih, b_hh,
                    epsilon, W1, b1, rms_weight, W2, b2, out):
    B, N, D = x.shape
    LAYERS = gru_weight.shape[0]
    H = W1.shape[1]
    CHUNKS = H // P
    COLS = GRAPHS * N
    ROUNDS = B // (GRAPHS * STREAMS)
    SPAN = LAYERS * STEP
    HALF = SPAN // 2
    RST, UPD, NEW = 0, 1, 2
    assert N == P and D == P and COLS == 512 and ROUNDS > 3

    x_v = x.rearrange("(k g) p d -> k p g d", g=GRAPHS)
    adj_v = adj.rearrange("(k g) p d -> k p g d", g=GRAPHS)
    out_v = out.rearrange("(k g) p d -> k p g d", g=GRAPHS)

    ctx = ExitStack()
    with ctx:
        def sb(name, shape, dt):
            return ctx.enter_context(nc.sbuf_tensor(name, shape, dt))

        def sem(name):
            return ctx.enter_context(nc.semaphore(name))

        def sem_pair(name):
            return [sem(f"{name}{s}") for s in range(STREAMS)]

        def buf(name, shape, dt=F32):
            return [sb(f"{name}{s}", [P] + shape, dt) for s in range(STREAMS)]

        ident = sb("ident", [P, P], F32)
        ident16 = sb("ident16", [P, P], F16)
        ones = sb("ones", [P, P], F32)
        minus_half = sb("minus_half", [P, GRAPHS], F32)
        w_ih_in = sb("w_ih_in", [P, 3, D], F32)
        w_hh_in = sb("w_hh_in", [P, 3, D], F32)
        gru_in = sb("gru_in", [P, LAYERS, D], F32)
        w_ihT = sb("w_ihT", [P, 3 * P], F32)
        w_hhT = sb("w_hhT", [P, 3 * P], F32)
        gruT = sb("gruT", [P, LAYERS, P], F32)
        w_state = sb("w_state", [P, 2, 3 * P], F16)
        w_agg = [sb(f"w_agg{l}", [P, 2, 3 * P], F16) for l in range(LAYERS)]
        bih_in = sb("bih_in", [P, 3], F32)
        bhh_in = sb("bhh_in", [P, 3], F32)
        gate_bias = sb("gate_bias", [P, 2], F32)
        hn_bias = sb("hn_bias", [P, 1], F32)
        w1_in = sb("w1_in", [P, H], F32)
        w1T = sb("w1T", [P, CHUNKS, P], F32)
        w1 = sb("w1", [P, 2, H], F16)
        gram = sb("gram", [P, 2, P], F16)
        gram_bias = sb("gram_bias", [P, 1], F32)
        b1_in = sb("b1_in", [P, CHUNKS], F32)
        b1_scaled = sb("b1_scaled", [P, CHUNKS], F32)
        b1_squares = sb("b1_squares", [P, CHUNKS], F32)
        b1_norm = sb("b1_norm", [P, 1], F32)
        rms_w = sb("rms_w", [P, CHUNKS], F32)
        rms_w_rows = sb("rms_w_rows", [P, H], F32)
        w1_rms = sb("w1_rms", [P, H], F32)
        w2_in = sb("w2_in", [P, CHUNKS, D], F32)
        w2 = sb("w2", [P, 2, CHUNKS, D], F16)
        b2_rows = sb("b2_rows", [P, D], F32)
        eps_col = sb("eps_col", [P, 1], F32)
        eps_ident = sb("eps_ident", [P, P], F32)
        mask_in = sb("mask_in", [B, N], F32)
        maskT = sb("maskT", [N, B], F32)

        adj_in = buf("adj_in", [GRAPHS, N])
        edges = buf("edges", [GRAPHS, N], F16)
        adjT = buf("adjT", [GRAPHS, N])
        state = buf("state", [COLS])
        state_parts = buf("state_parts", [2, COLS], F16)
        node_parts = buf("node_parts", [2, COLS], F16)
        agg_parts = buf("agg_parts", [2, COLS], F16)
        rgate = buf("rgate", [COLS])
        zgate = buf("zgate", [COLS])
        reset_hn = buf("reset_hn", [COLS])
        npre = buf("npre", [COLS])
        ncand = buf("ncand", [COLS])
        zstate = buf("zstate", [COLS])
        nmix = buf("nmix", [COLS])
        xout = buf("xout", [GRAPHS, D])

        def one(name, shape, dt=F32):
            return sb(name, [P] + shape, dt)

        ln_in = [one("xin", [GRAPHS, D]), one("x1", [GRAPHS, D])]
        ln_out = [one(f"ln_out{k}", [GRAPHS, D]) for k in range(2)]
        ln_stats = [one(f"ln_stats{k}", [GRAPHS, 6]) for k in range(2)]
        ln_mean2 = [one(f"ln_mean2{k}", [GRAPHS]) for k in range(2)]
        ln_diff = [one(f"ln_diff{k}", [GRAPHS]) for k in range(2)]
        ln_diff2 = [one(f"ln_diffsq{k}", [GRAPHS]) for k in range(2)]
        ln_sq = [one(f"ln_sq{k}", [GRAPHS]) for k in range(2)]
        ln_var = [one(f"ln_var{k}", [GRAPHS]) for k in range(2)]
        ln_rstd = [one(f"ln_rstd{k}", [GRAPHS]) for k in range(2)]
        ln_shift = [one(f"ln_shift{k}", [GRAPHS]) for k in range(2)]
        xin, x1 = ln_in
        node0_parts = one("first_node_parts", [2, COLS], F16)
        state0_parts = one("first_state_parts", [2, COLS], F16)
        state0 = one("first_state", [COLS])
        xres = one("xres", [GRAPHS, D])
        x1_b2 = one("x1_b2", [GRAPHS, D])
        sum_parts = one("sum_parts", [2, COLS], F16)
        sums = one("sums", [COLS])
        gram_prod = one("gram_prod", [COLS])
        mean_sq = one("mean_sq", [2, GRAPHS])
        rms = one("rms", [GRAPHS])
        rms_rows = one("rms_rows", [COLS])
        normed = [one(f"normed{c}", [COLS]) for c in range(CHUNKS)]
        sigm = [one(f"sigm{c}", [COLS]) for c in range(CHUNKS)]
        active = [one(f"active{c}", [COLS]) for c in range(CHUNKS)]
        active_parts = [one(f"active_parts{c}", [2, COLS], F16) for c in range(CHUNKS)]

        def bank(name):
            return ctx.enter_context(nc.psum_tensor(name, [P, COLS], F32))

        b_rz = [bank(f"b_rz{s}") for s in range(STREAMS)]
        b_h = [bank(f"b_h{s}") for s in range(STREAMS)]
        b_x = [bank(f"b_x{s}") for s in range(STREAMS)]
        b_p = bank("b_p")
        b_q = bank("b_q")
        banks = [[b_rz[0], b_h[0], b_x[0], b_p], [b_rz[1], b_h[1], b_x[1], b_q]]

        def half_view(bank):
            return bank[:, :].bitcast(F16).rearrange("p (a c) -> p a c", a=2)

        adj_loaded, stored = sem_pair("adj_loaded"), sem_pair("stored")
        edges_ready = sem_pair("edges_ready")
        turned_hi, turned_lo = sem_pair("turned_hi"), sem_pair("turned_lo")
        node_hi, node_lo = sem_pair("node_hi"), sem_pair("node_lo")
        agg_done, agg_hi, agg_lo = sem_pair("agg_done"), sem_pair("agg_hi"), sem_pair("agg_lo")
        r_done, z_done, hn_done, in_done = (sem_pair("r_done"), sem_pair("z_done"),
                                            sem_pair("hn_done"), sem_pair("in_done"))
        r_ready, z_ready = sem_pair("r_ready"), sem_pair("z_ready")
        rhn_ready, npre_ready, n_ready = sem_pair("rhn_ready"), sem_pair("npre_ready"), sem_pair("n_ready")
        zh_ready, nmix_ready, h_ready = sem_pair("zh_ready"), sem_pair("nmix_ready"), sem_pair("h_ready")
        h_hi, h_lo = sem_pair("h_hi"), sem_pair("h_lo")
        xin_loaded, xres_loaded = sem("xin_loaded"), sem("xres_loaded")
        stats_done, mv_done, diff_done = sem_pair("stats_done"), sem_pair("mv_done"), sem_pair("diff_done")
        var_ready, rstd_ready = sem_pair("var_ready"), sem_pair("rstd_ready")
        shift_ready, norm_ready = sem_pair("shift_ready"), sem_pair("norm_ready")
        node0_hi, node0_ready = sem("node0_hi"), sem("node0_ready")
        state0_turned, state0_parts_ready, state0_ready = (sem("state0_turned"), sem("state0_parts_ready"),
                                                           sem("state0_ready"))
        adj_turned, adjT_ready = sem("adj_turned"), sem("adjT_ready")
        back_done, x1_ready, x1b2_ready = sem("back_done"), sem("x1_ready"), sem("x1b2_ready")
        sums_done, sums_hi, sums_ready, sums_lo = (sem("sums_done"), sem("sums_hi"),
                                                   sem("sums_ready"), sem("sums_lo"))
        gram_done, gprod_ready, ms_done = sem("gram_done"), sem("gprod_ready"), sem("ms_done")
        ms_read, ms_ready, rms_ready = sem("ms_read"), sem("ms_ready"), sem("rms_ready")
        rows_done, rows_ready = sem("rows_done"), sem("rows_ready")
        chunk_done, normed_ready, sigm_ready = sem("chunk_done"), sem("normed_ready"), sem("sigm_ready")
        active_ready, active_hi, active_lo = sem("active_ready"), sem("active_hi"), sem("active_lo")
        out_done, xout_ready = sem("out_done"), sem("xout_ready")
        params_loaded, w_loaded = sem("params_loaded"), sem("w_loaded")
        ident_zero, consts_ready = sem("ident_zero"), sem("consts_ready")
        ident16_ready = sem("ident16_ready")
        w_turned, w_copied, w_product, setup_chain, weights_ready = (
            sem("w_turned"), sem("w_copied"), sem("w_product"), sem("setup_chain"), sem("weights_ready"))
        w1w_ready = sem("w1w_ready")

        def schedule(eng, layer, tail, prepare):
            def stream(s, n, t):
                layer(s, n, t // STEP, t % STEP)

            for q in range(HALF):
                prepare(0, 0, q)
            for t in range(HALF):
                stream(0, 0, t)
                prepare(1, 0, t)
            for t in range(HALF):
                stream(0, 0, t + HALF)
                stream(1, 0, t)
                prepare(0, 1, t)
            with eng.Fori(1, ROUNDS - 1) as i:
                for t in range(HALF):
                    stream(0, i, t)
                    stream(1, i - 1, t + HALF)
                    tail(0, i - 1, t, i)
                    prepare(1, i, t)
                for t in range(HALF):
                    stream(0, i, t + HALF)
                    stream(1, i, t)
                    tail(1, i - 1, t, i)
                    prepare(0, i + 1, t)
            last = ROUNDS - 1
            for t in range(HALF):
                stream(0, last, t)
                stream(1, last - 1, t + HALF)
                tail(0, last - 1, t, last)
                prepare(1, last, t)
            for t in range(HALF):
                stream(0, last, t + HALF)
                stream(1, last, t)
                tail(1, last - 1, t, last)
            for t in range(HALF):
                stream(1, last, t + HALF)
                tail(0, last, t, None)
            for t in range(HALF):
                tail(1, last, t, None)

        def order(s, n):
            return STREAMS * n + s

        def at(q, step):
            return q == AT_TAIL[step]

        def at_layer(q, step):
            return q == AT_LAYER[step]

        block = ctx.enter_context(nc.Block())

        @block.sync
        def _(sp):
            def load_xin(s, n):
                sp.dma_start(xin[:, :, :], x_v[STREAMS * n + 1 - s]).then_inc(xin_loaded, 16)

            def load_xres(s, n):
                sp.dma_start(xres[:, :, :], x_v[STREAMS * n + 1 - s]).then_inc(xres_loaded, 16)

            def load_adj(s, n):
                sp.dma_start(adj_in[s][:, :, :], adj_v[STREAMS * n + 1 - s]).then_inc(adj_loaded[s], 16)

            sp.dma_start(w_ih_in[:, :, :], w_ih.rearrange("(g p) e -> p g e", p=P)).then_inc(w_loaded, 16)
            sp.dma_start(gru_in[:, :, :], gru_weight.rearrange("l d e -> d l e")).then_inc(w_loaded, 16)
            sp.dma_start(w_hh_in[:, :, :], w_hh.rearrange("(g p) e -> p g e", p=P)).then_inc(w_loaded, 16)
            sp.dma_start(w1_in[:, :], W1).then_inc(w_loaded, 16)
            sp.dma_start(mask_in[:, :], nodemask).then_inc(w_loaded, 16)
            load_xin(0, 0)
            load_adj(0, 0)
            sp.dma_start(w2_in[:, :, :], W2.rearrange("(c p) d -> p c d", p=P)).then_inc(params_loaded, 16)
            with nc.allow_non_contiguous_dma(reason="bias columns of a few hundred numbers, once"):
                sp.dma_start(bih_in[:, :], b_ih.rearrange("(g p) -> p g", p=P)).then_inc(params_loaded, 16)
                sp.dma_start(bhh_in[:, :], b_hh.rearrange("(g p) -> p g", p=P)).then_inc(params_loaded, 16)
                sp.dma_start(b1_in[:, :], b1.rearrange("(c p) -> p c", p=P)).then_inc(params_loaded, 16)
                sp.dma_start(rms_w[:, :], rms_weight.rearrange("(c p) -> p c", p=P)).then_inc(params_loaded, 16)
            sp.dma_start(rms_w_rows[:, :], rms_weight.partition_broadcast(P)).then_inc(params_loaded, 16)
            sp.dma_start(b2_rows[:, :], b2.partition_broadcast(P)).then_inc(params_loaded, 16)
            sp.dma_start(eps_col[:, :], epsilon.partition_broadcast(P)).then_inc(params_loaded, 16)
            load_adj(1, 0)
            load_xres(0, 0)

            def layer(s, n, l, q):
                pass

            def tail(s, n, q, nxt):
                m = order(s, n)
                if at(q, "load_res") and not (s == 1 and nxt is None):
                    sp.wait_ge(x1_ready, m + 1)
                    load_xres(1 - s, n if s == 0 else nxt)
                if at(q, "store"):
                    sp.wait_ge(xout_ready, m + 2)
                    sp.dma_start(out_v[STREAMS * n + 1 - s], xout[s][:, :, :]).then_inc(stored[s], 16)

            def prepare(s, n, q):
                last_one = s == 1 and isinstance(n, int) and n == ROUNDS - 1
                if at(q, "load_x") and not last_one:
                    sp.wait_ge(norm_ready[0], GRAPHS * order(s, n) + GRAPHS)
                    load_xin(1 - s, n if s == 0 else n + 1)
                if at(q, "load_adj") and not (isinstance(n, int) and n == 0):
                    sp.wait_ge(edges_ready[s], n)
                    sp.wait_ge(adj_turned, order(s, n - 1) + 1)
                    load_adj(s, n)

            schedule(sp, layer, tail, prepare)
            for s in range(STREAMS):
                sp.wait_ge(stored[s], 16 * ROUNDS + 16)

        @block.gpsimd
        def _(pool):
            pool.memset(ident[:, :], 0.0).then_inc(ident_zero, 1)
            pool.memset(ones[:, :], 1.0)
            pool.memset(minus_half[:, :], -0.5)
            pool.wait_ge(ident_zero, 1)
            pool.affine_select(out=ident[:, :], in_=ident[:, :], compare_op=ALU.not_equal, fill=1.0, base=0,
                               pattern=[[-1, P]], channel_multiplier=1).then_inc(consts_ready, 1)
            pool.wait_ge(consts_ready, 1)

            def rstd(m, k):
                pool.wait_ge(var_ready[k], m + 1)
                pool.tensor_tensor(ln_rstd[k][:, :], ln_var[k][:, :], minus_half[:, :], ALU.pow)\
                    .then_inc(rstd_ready[k], 1)

            def layer(s, n, l, q):
                if at_layer(q, "state_lo"):
                    pool.wait_ge(h_hi[s], LAYERS * n + l + 1)
                    pool.tensor_tensor(state_parts[s][:, LO, :], state[s][:, :], state_parts[s][:, HI, :],
                                       ALU.subtract).then_inc(h_lo[s], 1)

            def tail(s, n, q, nxt):
                m = order(s, n)
                if at(q, "x1_b2"):
                    pool.wait_ge(x1_ready, m + 1)
                    pool.tensor_tensor(x1_b2[:, :, :], x1[:, :, :],
                                       b2_rows[:, :].unsqueeze(1).to_broadcast([P, GRAPHS, D]), ALU.add)\
                        .then_inc(x1b2_ready, 1)
                if at(q, "pow1"):
                    rstd(m, 1)
                if at(q, "pow_ms"):
                    pool.wait_ge(ms_ready, m + 1)
                    pool.tensor_tensor(rms[:, :], mean_sq[:, 1, :], minus_half[:, :], ALU.pow)\
                        .then_inc(rms_ready, 1)
                for c in range(CHUNKS):
                    if at(q, f"silu{c}"):
                        pool.wait_ge(sigm_ready, CHUNKS * m + c + 1)
                        pool.tensor_tensor(active[c][:, :], normed[c][:, :], sigm[c][:, :], ALU.mult)\
                            .then_inc(active_ready, 1)
                    if at(q, f"lo{c}"):
                        pool.wait_ge(active_hi, CHUNKS * m + c + 1)
                        pool.tensor_tensor(active_parts[c][:, LO, :], active[c][:, :],
                                           active_parts[c][:, HI, :], ALU.subtract).then_inc(active_lo, 1)

            def prepare(s, n, q):
                if at(q, "pow0"):
                    rstd(order(s, n), 0)
                if at(q, "state0"):
                    pool.wait_ge(state0_parts_ready, order(s, n) + 1)
                    pool.tensor_tensor(state0[:, :], state0_parts[:, HI, :], state0_parts[:, LO, :], ALU.add)\
                        .then_inc(state0_ready, 1)

            pool.wait_ge(params_loaded, 16 * 8)
            schedule(pool, layer, tail, prepare)

        @block.scalar
        def _(act):
            act.preload_act_table_set("sigmoid_and_others")

            def normalize(m, k):
                act.wait_ge(shift_ready[k], m + 1)
                for g in range(GRAPHS):
                    act.activation(ln_out[k][:, g, :], ln_in[k][:, g, :], ACT.Relu, bias=ln_shift[k][:, g:g + 1],
                                   scale=ln_rstd[k][:, g:g + 1]).then_inc(norm_ready[k], 1)

            def layer(s, n, l, q):
                k = LAYERS * n + l + 1
                if at_layer(q, "copy_hi") and l > 0:
                    act.wait_ge(turned_hi[s], (LAYERS - 1) * n + l)
                    act.activation(node_parts[s][:, HI, :], half_view(b_x[s])[:, HI, :], ACT.Copy)\
                        .then_inc(node_hi[s], 1)
                if at_layer(q, "copy_lo") and l > 0:
                    act.wait_ge(turned_lo[s], (LAYERS - 1) * n + l)
                    act.activation(node_parts[s][:, LO, :], half_view(b_h[s])[:, LO, :], ACT.Copy)\
                        .then_inc(node_lo[s], 1)
                if at_layer(q, "agg_hi"):
                    act.wait_ge(agg_done[s], k)
                    act.activation(agg_parts[s][:, HI, :], b_x[s][:, :], ACT.Copy).then_inc(agg_hi[s], 1)
                if at_layer(q, "sigmoid_r"):
                    act.wait_ge(r_done[s], k)
                    act.activation(rgate[s][:, :], b_rz[s][:, :], ACT.Sigmoid, bias=gate_bias[:, RST:RST + 1],
                                   scale=1.0 / GATE_SCALE).then_inc(r_ready[s], 1)
                if at_layer(q, "sigmoid_z"):
                    act.wait_ge(z_done[s], k)
                    act.activation(zgate[s][:, :], b_rz[s][:, :], ACT.Sigmoid, bias=gate_bias[:, UPD:UPD + 1],
                                   scale=1.0 / GATE_SCALE).then_inc(z_ready[s], 1)
                if at_layer(q, "tanh"):
                    act.wait_ge(npre_ready[s], k)
                    act.activation(ncand[s][:, :], npre[s][:, :], ACT.Tanh, bias=bih_in[:, NEW:NEW + 1],
                                   scale=1.0 / GATE_SCALE).then_inc(n_ready[s], 1)
                if at_layer(q, "state_hi"):
                    if l == 0 and not (isinstance(n, int) and n == 0):
                        act.wait_ge(back_done, order(s, n - 1) + 1)
                    act.wait_ge(h_ready[s], k)
                    act.activation(state_parts[s][:, HI, :], state[s][:, :], ACT.Copy).then_inc(h_hi[s], 1)

            def tail(s, n, q, nxt):
                m = order(s, n)
                if at(q, "relu1"):
                    normalize(m, 1)
                if at(q, "sums_hi"):
                    act.wait_ge(sums_done, m + 1)
                    act.activation(sum_parts[:, HI, :], b_q[:, :], ACT.Copy, scale=AGG_SCALE).then_inc(sums_hi, 1)
                    act.activation(sums[:, :], b_q[:, :], ACT.Copy).then_inc(sums_ready, 1)
                if at(q, "copy_rows"):
                    act.wait_ge(rows_done, m + 1)
                    act.activation(rms_rows[:, :], b_p[:, :], ACT.Copy, scale=ACTIVE_SCALE).then_inc(rows_ready, 1)
                for c in range(CHUNKS):
                    if at(q, f"sigmoid{c}"):
                        act.wait_ge(normed_ready, CHUNKS * m + c + 1)
                        act.activation(sigm[c][:, :], normed[c][:, :], ACT.Sigmoid, scale=1.0 / ACTIVE_SCALE)\
                            .then_inc(sigm_ready, 1)
                    if at(q, f"hi{c}"):
                        act.wait_ge(active_ready, CHUNKS * m + c + 1)
                        act.activation(active_parts[c][:, HI, :], active[c][:, :], ACT.Copy).then_inc(active_hi, 1)

            def prepare(s, n, q):
                m = order(s, n)
                if at(q, "relu0"):
                    normalize(m, 0)
                if at(q, "node_hi0"):
                    act.wait_ge(norm_ready[0], GRAPHS * m + GRAPHS)
                    act.activation(node0_parts[:, HI, :].rearrange("p (g d) -> p g d", g=GRAPHS),
                                   ln_out[0][:, :, :], ACT.Copy, scale=STATE_SCALE).then_inc(node0_hi, 1)

            schedule(act, layer, tail, prepare)

        @block.vector
        def _(dve):
            chain = [0]

            def link(ins):
                chain[0] += 1
                ins.then_inc(setup_chain, 1)
                dve.wait_ge(setup_chain, chain[0])

            def split(dst_hi, dst_lo, src, scale):
                link(dve.tensor_scalar(dst_hi, src, scale, None, ALU.mult))
                return dve.scalar_tensor_tensor(out=dst_lo, in0=src, scalar=scale, in1=dst_hi,
                                                op0=ALU.mult, op1=ALU.subtract)

            def setup():
                dve.wait_ge(consts_ready, 1)
                dve.tensor_copy(ident16[:, :], ident[:, :]).then_inc(ident16_ready, 1)
                dve.wait_ge(w_turned, 1)
                dve.tensor_copy(w_ihT[:, :], banks[0][0][:, 0:3 * P])
                dve.tensor_copy(gruT[:, 0:4, :], banks[0][1][:, :].rearrange("p (l d) -> p l d", l=4))
                dve.tensor_copy(gruT[:, 4, :], banks[0][2][:, 0:P])
                dve.tensor_copy(w1T[:, :, :], banks[0][3][:, :].rearrange("p (c d) -> p c d", c=CHUNKS))
                dve.tensor_scalar(maskT[:, :], banks[1][1][:, 0:B], 1.0 / STATE_SCALE, None, ALU.mult)
                split(w_state[:, HI, :], w_state[:, LO, :], banks[1][0][:, 0:3 * P], WEIGHT_SCALE)\
                    .then_inc(w_copied, 1)
                dve.wait_ge(params_loaded, 16 * 8)
                link(dve.tensor_tensor(b1_squares[:, :], b1_in[:, :], b1_in[:, :], ALU.mult))
                dve.tensor_scalar(eps_ident[:, :], ident[:, :], eps_col[:, 0:1], None, ALU.mult)\
                    .then_inc(w_copied, 1)
                dve.tensor_tensor(gate_bias[:, :], bih_in[:, 0:2], bhh_in[:, 0:2], ALU.add).then_inc(stored[0], 16)
                dve.tensor_scalar(hn_bias[:, :], bhh_in[:, NEW:NEW + 1], GATE_SCALE, None, ALU.mult)\
                    .then_inc(stored[1], 16)
                dve.scalar_tensor_tensor(out=b1_scaled[:, :], in0=b1_in[:, :], scalar=AGG_SCALE * WEIGHT_SCALE,
                                         in1=rms_w[:, :], op0=ALU.mult, op1=ALU.mult).then_inc(xout_ready, 1)
                link(dve.tensor_tensor(w1_rms[:, :], w1_in[:, :], rms_w_rows[:, :], ALU.mult))
                split(w1[:, HI, :], w1[:, LO, :], w1_rms[:, :], WEIGHT_SCALE)
                split(w2[:, HI, :, :], w2[:, LO, :, :], w2_in[:, :, :], WEIGHT_SCALE)
                dve.wait_ge(w_product, 1)
                spots = [banks[0][0], banks[0][1], banks[0][2], banks[0][3], banks[1][0]]
                for l in range(LAYERS):
                    split(w_agg[l][:, HI, :], w_agg[l][:, LO, :], spots[l][:, 0:3 * P], WEIGHT_SCALE)
                split(gram[:, HI, :], gram[:, LO, :], banks[1][1][:, 0:P], GRAM_SCALE)
                dve.tensor_scalar(gram_bias[:, :], banks[1][2][:, 0:1], 2.0 * GRAM_SCALE * AGG_SCALE, None, ALU.mult)
                dve.tensor_scalar(b1_norm[:, :], banks[1][3][:, 0:1],
                                  (AGG_SCALE * WEIGHT_SCALE) ** 2 / H, None, ALU.mult).then_inc(weights_ready, 1)

            def statistics(m, k):
                if k == 0:
                    dve.wait_ge(xin_loaded, 16 * m + 16)
                else:
                    dve.wait_ge(x1_ready, m + 1)
                for g in range(GRAPHS):
                    ins = dve.bn_stats(ln_stats[k][:, g, :], ln_in[k][:, g, :])
                ins.then_inc(stats_done[k], 1)
                dve.wait_ge(stats_done[k], m + 1)
                st = ln_stats[k]
                dve.tensor_tensor(ln_diff[k][:, :], st[:, :, 1], st[:, :, 4], ALU.subtract).then_inc(mv_done[k], 1)
                dve.tensor_tensor(ln_mean2[k][:, :], st[:, :, 1], st[:, :, 4], ALU.add)
                dve.scalar_tensor_tensor(out=ln_sq[k][:, :], in0=st[:, :, 2], scalar=LN_EPS * D,
                                         in1=st[:, :, 5], op0=ALU.add, op1=ALU.add)
                dve.wait_ge(mv_done[k], m + 1)
                dve.scalar_tensor_tensor(out=ln_diff2[k][:, :], in0=ln_diff[k][:, :], scalar=0.25,
                                         in1=ln_diff[k][:, :], op0=ALU.mult, op1=ALU.mult).then_inc(diff_done[k], 1)
                dve.wait_ge(diff_done[k], m + 1)
                dve.scalar_tensor_tensor(out=ln_var[k][:, :], in0=ln_sq[k][:, :], scalar=1.0 / D,
                                         in1=ln_diff2[k][:, :], op0=ALU.mult, op1=ALU.add)\
                    .then_inc(var_ready[k], 1)

            def shift(m, k):
                dve.wait_ge(rstd_ready[k], m + 1)
                dve.scalar_tensor_tensor(out=ln_shift[k][:, :], in0=ln_mean2[k][:, :], scalar=-0.5,
                                         in1=ln_rstd[k][:, :], op0=ALU.mult, op1=ALU.mult)\
                    .then_inc(shift_ready[k], 1)

            def take_edges(s, n):
                dve.wait_ge(adj_loaded[s], 16 * n + 16)
                dve.tensor_scalar(edges[s][:, :, :], adj_in[s][:, :, :], 0.0, None, ALU.not_equal)\
                    .then_inc(edges_ready[s], 1)

            def add_epsilon(s, m):
                dve.wait_ge(adj_turned, m + 1)
                dve.tensor_tensor(adjT[s][:, :, :], b_q[:, :].rearrange("p (g d) -> p g d", g=GRAPHS),
                                  eps_ident[:, :].unsqueeze(1).to_broadcast([P, GRAPHS, N]), ALU.add)\
                    .then_inc(adjT_ready, 1)

            def layer(s, n, l, q):
                k = LAYERS * n + l + 1
                if at_layer(q, "agg_lo"):
                    dve.wait_ge(agg_hi[s], k)
                    dve.tensor_tensor(agg_parts[s][:, LO, :], b_x[s][:, :], agg_parts[s][:, HI, :], ALU.subtract)\
                        .then_inc(agg_lo[s], 1)
                if at_layer(q, "reset"):
                    dve.wait_ge(r_ready[s], k)
                    dve.wait_ge(hn_done[s], k)
                    dve.scalar_tensor_tensor(out=reset_hn[s][:, :], in0=b_h[s][:, :], scalar=hn_bias[:, 0:1],
                                             in1=rgate[s][:, :], op0=ALU.add, op1=ALU.mult)\
                        .then_inc(rhn_ready[s], 1)
                if at_layer(q, "add_input"):
                    dve.wait_ge(rhn_ready[s], k)
                    dve.wait_ge(in_done[s], k)
                    dve.tensor_tensor(npre[s][:, :], b_x[s][:, :], reset_hn[s][:, :], ALU.add)\
                        .then_inc(npre_ready[s], 1)
                if at_layer(q, "z_state"):
                    dve.wait_ge(z_ready[s], k)
                    if l == 0:
                        dve.wait_ge(state0_ready, order(s, n) + 1)
                    old = state0 if l == 0 else state[s]
                    dve.tensor_tensor(zstate[s][:, :], zgate[s][:, :], old[:, :], ALU.mult)\
                        .then_inc(zh_ready[s], 1)
                if at_layer(q, "mix"):
                    dve.wait_ge(n_ready[s], k)
                    dve.wait_ge(z_ready[s], k)
                    dve.scalar_tensor_tensor(out=nmix[s][:, :], in0=zgate[s][:, :], scalar=-1.0, in1=ncand[s][:, :],
                                             op0=ALU.add, op1=ALU.mult).then_inc(nmix_ready[s], 1)
                if at_layer(q, "new_state"):
                    dve.wait_ge(nmix_ready[s], k)
                    dve.wait_ge(zh_ready[s], k)
                    dve.scalar_tensor_tensor(out=state[s][:, :], in0=nmix[s][:, :], scalar=-STATE_SCALE,
                                             in1=zstate[s][:, :], op0=ALU.mult, op1=ALU.add)\
                        .then_inc(h_ready[s], 1)
                if at_layer(q, "edges") and l == LAYERS - 1 and not (isinstance(n, int) and n == ROUNDS - 1):
                    dve.wait_ge(agg_done[s], k)
                    take_edges(s, n + 1)

            def tail(s, n, q, nxt):
                m = order(s, n)
                if at(q, "x1"):
                    dve.wait_ge(back_done, m + 1)
                    dve.wait_ge(xres_loaded, 16 * m + 16)
                    first = (n * STREAMS + 1 - s) * GRAPHS
                    for g in range(GRAPHS):
                        ins = dve.scalar_tensor_tensor(out=x1[:, g, :], in0=b_p[:, g * P:(g + 1) * P],
                                                       scalar=maskT[:, bass.ds(first + g, 1)], in1=xres[:, g, :],
                                                       op0=ALU.mult, op1=ALU.add)
                    ins.then_inc(x1_ready, 1)
                if at(q, "stats1"):
                    statistics(m, 1)
                if at(q, "shift1"):
                    shift(m, 1)
                if at(q, "sums_lo"):
                    dve.wait_ge(sums_hi, m + 1)
                    dve.wait_ge(sums_ready, m + 1)
                    dve.scalar_tensor_tensor(out=sum_parts[:, LO, :], in0=b_q[:, :], scalar=AGG_SCALE,
                                             in1=sum_parts[:, HI, :], op0=ALU.mult, op1=ALU.subtract)\
                        .then_inc(sums_lo, 1)
                if at(q, "gram_prod"):
                    dve.wait_ge(gram_done, m + 1)
                    dve.scalar_tensor_tensor(out=gram_prod[:, :], in0=b_p[:, :], scalar=gram_bias[:, 0:1],
                                             in1=sums[:, :], op0=ALU.add, op1=ALU.mult).then_inc(gprod_ready, 1)
                if at(q, "mean_sq_read"):
                    dve.wait_ge(ms_done, m + 1)
                    dve.tensor_scalar(mean_sq[:, 0, :], b_q[:, 0:GRAPHS],
                                      AGG_SCALE * WEIGHT_SCALE ** 2 / (GRAM_SCALE * H), b1_norm[:, 0:1],
                                      ALU.mult, ALU.add).then_inc(ms_read, 1)
                    dve.wait_ge(ms_read, m + 1)
                    dve.tensor_scalar(mean_sq[:, 1, :], mean_sq[:, 0, :], 0.0,
                                      RMS_EPS * (AGG_SCALE * WEIGHT_SCALE) ** 2, ALU.max, ALU.add)\
                        .then_inc(ms_ready, 1)
                for c in range(CHUNKS):
                    if at(q, f"norm{c}"):
                        if c == 0:
                            dve.wait_ge(rows_ready, m + 1)
                        dve.wait_ge(chunk_done, CHUNKS * m + c + 1)
                        dve.scalar_tensor_tensor(out=normed[c][:, :], in0=b_q[:, :], scalar=b1_scaled[:, c:c + 1],
                                                 in1=rms_rows[:, :], op0=ALU.add, op1=ALU.mult)\
                            .then_inc(normed_ready, 1)
                if at(q, "add_epsilon") and nxt is not None:
                    add_epsilon(s, order(s, nxt))
                if at(q, "out"):
                    dve.wait_ge(stored[s], 16 * n + 16)
                    dve.wait_ge(x1b2_ready, m + 1)
                    dve.wait_ge(out_done, m + 1)
                    dve.scalar_tensor_tensor(out=xout[s][:, :, :],
                                             in0=b_p[:, :].rearrange("p (g d) -> p g d", g=GRAPHS),
                                             scalar=1.0 / (ACTIVE_SCALE * WEIGHT_SCALE), in1=x1_b2[:, :, :],
                                             op0=ALU.mult, op1=ALU.add).then_inc(xout_ready, 1)

            def prepare(s, n, q):
                m = order(s, n)
                if at(q, "stats0"):
                    statistics(m, 0)
                if at(q, "shift0"):
                    shift(m, 0)
                if at(q, "node_lo0"):
                    dve.wait_ge(node0_hi, m + 1)
                    dve.scalar_tensor_tensor(out=node0_parts[:, LO, :].rearrange("p (g d) -> p g d", g=GRAPHS),
                                             in0=ln_out[0][:, :, :], scalar=STATE_SCALE,
                                             in1=node0_parts[:, HI, :].rearrange("p (g d) -> p g d", g=GRAPHS),
                                             op0=ALU.mult, op1=ALU.subtract).then_inc(node0_ready, 1)
                if at(q, "copy_state0"):
                    dve.wait_ge(state0_turned, m + 1)
                    dve.tensor_copy(state0_parts[:, :, :], half_view(b_q)).then_inc(state0_parts_ready, 1)

            setup()
            for s in range(STREAMS):
                take_edges(s, 0)
                add_epsilon(s, s)
            schedule(dve, layer, tail, prepare)

        @block.tensor
        def _(pe):
            def setup():
                pe.wait_ge(consts_ready, 1)
                pe.wait_ge(w_loaded, 16 * 5)
                for g in range(3):
                    pe.transpose(banks[0][0][:, g * P:(g + 1) * P], w_ih_in[:, g, :], ident[:, :])
                    pe.transpose(banks[1][0][:, g * P:(g + 1) * P], w_hh_in[:, g, :], ident[:, :])
                for l in range(LAYERS):
                    pe.transpose(banks[0][1 + l // 4][:, (l % 4) * P:(l % 4 + 1) * P], gru_in[:, l, :], ident[:, :])
                for c in range(CHUNKS):
                    pe.transpose(banks[0][3][:, c * P:(c + 1) * P], w1_in[:, c * P:(c + 1) * P], ident[:, :])
                pe.transpose(banks[1][1][:, 0:B], mask_in[:, :], ident[:, :]).then_inc(w_turned, 1)
                pe.wait_ge(w_copied, 2)
                spots = [banks[0][0], banks[0][1], banks[0][2], banks[0][3], banks[1][0]]
                for l in range(LAYERS):
                    pe.matmul(spots[l][:, 0:3 * P], gruT[:, l, :], w_ihT[:, :], start=True, stop=True)
                for c in range(CHUNKS):
                    pe.matmul(banks[1][1][:, 0:P], w1T[:, c, :], w1T[:, c, :], start=(c == 0), stop=(c == CHUNKS - 1))
                for c in range(CHUNKS):
                    pe.matmul(banks[1][2][:, 0:1], w1T[:, c, :], b1_in[:, c:c + 1],
                              start=(c == 0), stop=(c == CHUNKS - 1))
                for c in range(CHUNKS):
                    ins = pe.matmul(banks[1][3][:, 0:1], ones[:, :], b1_squares[:, c:c + 1],
                                    start=(c == 0), stop=(c == CHUNKS - 1))
                ins.then_inc(w_product, 1)
                pe.wait_ge(weights_ready, 1)

            def turn_adj(s, n):
                pe.wait_ge(adj_loaded[s], 16 * n + 16)
                for g in range(GRAPHS):
                    ins = pe.transpose(b_q[:, g * P:(g + 1) * P], adj_in[s][:, g, :], ident[:, :])
                ins.then_inc(adj_turned, 1)

            def gate(out, w, g, parts, which, first, last):
                for k, (wp, ap) in enumerate(which):
                    ins = pe.matmul(out[:, :], w[:, wp, g * P:(g + 1) * P], parts[:, ap, :],
                                    start=(first and k == 0), stop=(last and k == len(which) - 1))
                return ins

            OF_HI = ((HI, HI), (LO, HI))
            OF_LO = ((HI, LO),)
            ALL = OF_HI + OF_LO

            def turn(bank, parts, part):
                for g in range(GRAPHS):
                    ins = pe.transpose(half_view(bank)[:, part, g * P:(g + 1) * P],
                                       parts[:, part, g * P:(g + 1) * P], ident16[:, :])
                return ins

            def aggregate(bank, nodes, part, graph_edges):
                for g in range(GRAPHS):
                    ins = pe.matmul(bank[:, g * P:(g + 1) * P], nodes[:, part, g * P:(g + 1) * P],
                                    graph_edges[:, g, :], start=(part == HI and g == 0), stop=(part == LO),
                                    skip_group_check=True)
                return ins

            def layer(s, n, l, q):
                k = LAYERS * n + l + 1
                old = state0_parts if l == 0 else state_parts[s]
                nodes = node0_parts if l == 0 else node_parts[s]
                if at_layer(q, "turn_hi") and l > 0:
                    pe.wait_ge(h_hi[s], k - 1)
                    turn(b_x[s], state_parts[s], HI).then_inc(turned_hi[s], 1)
                if at_layer(q, "hidden_r_hi"):
                    if l == 0:
                        pe.wait_ge(state0_parts_ready, order(s, n) + 1)
                    gate(b_rz[s], w_state, RST, old, OF_HI, True, False)
                if at_layer(q, "turn_lo") and l > 0:
                    pe.wait_ge(h_lo[s], k - 1)
                    turn(b_h[s], state_parts[s], LO).then_inc(turned_lo[s], 1)
                if at_layer(q, "hidden_r_lo"):
                    gate(b_rz[s], w_state, RST, old, OF_LO, False, False)
                if at_layer(q, "agg_of_hi"):
                    if l == 0:
                        pe.wait_ge(edges_ready[s], n + 1)
                    else:
                        pe.wait_ge(node_hi[s], (LAYERS - 1) * n + l)
                    aggregate(b_x[s], nodes, HI, edges[s])
                if at_layer(q, "agg_of_lo"):
                    if l > 0:
                        pe.wait_ge(node_lo[s], (LAYERS - 1) * n + l)
                    aggregate(b_x[s], nodes, LO, edges[s]).then_inc(agg_done[s], 1)
                if at_layer(q, "hidden_n"):
                    gate(b_h[s], w_state, NEW, old, ALL, True, True).then_inc(hn_done[s], 1)
                if at_layer(q, "input_r"):
                    pe.wait_ge(agg_hi[s], k)
                    gate(b_rz[s], w_agg[l], RST, agg_parts[s], OF_HI, False, False)
                    pe.wait_ge(agg_lo[s], k)
                    gate(b_rz[s], w_agg[l], RST, agg_parts[s], OF_LO, False, True).then_inc(r_done[s], 1)
                if at_layer(q, "input_n"):
                    gate(b_x[s], w_agg[l], NEW, agg_parts[s], ALL, True, True).then_inc(in_done[s], 1)
                if at_layer(q, "gate_z"):
                    pe.wait_ge(r_ready[s], k)
                    gate(b_rz[s], w_state, UPD, old, ALL, True, False)
                    gate(b_rz[s], w_agg[l], UPD, agg_parts[s], ALL, False, True).then_inc(z_done[s], 1)

            def tail(s, n, q, nxt):
                m = order(s, n)
                if at(q, "back"):
                    pe.wait_ge(xout_ready, m + 1)
                    pe.wait_ge(h_hi[s], LAYERS * n + LAYERS)
                    pe.wait_ge(h_lo[s], LAYERS * n + LAYERS)
                    for g in range(GRAPHS):
                        for part in (HI, LO):
                            ins = pe.matmul(b_p[:, g * P:(g + 1) * P], state_parts[s][:, part, g * P:(g + 1) * P],
                                            ident16[:, :], start=(part == HI), stop=(part == LO))
                    ins.then_inc(back_done, 1)
                if at(q, "sums"):
                    if nxt is not None:
                        pe.wait_ge(state0_parts_ready, m + 3)
                    else:
                        pe.wait_ge(adjT_ready, min(m + 2, STREAMS * ROUNDS))
                        pe.wait_ge(normed_ready, CHUNKS * m)
                    pe.wait_ge(adjT_ready, m + 1)
                    for g in range(GRAPHS):
                        pe.wait_ge(norm_ready[1], GRAPHS * m + g + 1)
                        ins = pe.matmul(b_q[:, g * P:(g + 1) * P], ln_out[1][:, g, :], adjT[s][:, g, :],
                                        start=True, stop=True)
                    ins.then_inc(sums_done, 1)
                if at(q, "gram"):
                    pe.wait_ge(sums_hi, m + 1)
                    for part in (HI, LO):
                        pe.matmul(b_p[:, :], gram[:, part, :], sum_parts[:, HI, :], start=(part == HI), stop=False)
                    pe.wait_ge(sums_lo, m + 1)
                    pe.matmul(b_p[:, :], gram[:, HI, :], sum_parts[:, LO, :], start=False, stop=True)\
                        .then_inc(gram_done, 1)
                if at(q, "mean_sq"):
                    pe.wait_ge(gprod_ready, m + 1)
                    for g in range(GRAPHS):
                        ins = pe.matmul(b_q[:, g:g + 1], gram_prod[:, g * P:(g + 1) * P], ones[:, 0:1],
                                        start=True, stop=True)
                    ins.then_inc(ms_done, 1)
                if at(q, "rows"):
                    pe.wait_ge(rms_ready, m + 1)
                    for g in range(GRAPHS):
                        ins = pe.transpose(b_p[:, g * P:(g + 1) * P], rms[:, g:g + 1].to_broadcast([P, P]),
                                           ident[:, :])
                    ins.then_inc(rows_done, 1)
                for c in range(CHUNKS):
                    if at(q, f"chunk{c}"):
                        if c == 0:
                            pe.wait_ge(ms_read, m + 1)
                        else:
                            pe.wait_ge(normed_ready, CHUNKS * m + c)
                        gate(b_q, w1, c, sum_parts, ALL, True, True).then_inc(chunk_done, 1)
                    if at(q, f"project{c}"):
                        if c == 0:
                            pe.wait_ge(rows_ready, m + 1)
                        for part, ready in ((HI, active_hi), (LO, active_lo)):
                            pe.wait_ge(ready, CHUNKS * m + c + 1)
                            for g in range(GRAPHS):
                                for wp in ((HI, LO) if part == HI else (HI,)):
                                    ins = pe.matmul(b_p[:, g * P:(g + 1) * P],
                                                    active_parts[c][:, part, g * P:(g + 1) * P], w2[:, wp, c, :],
                                                    start=(c == 0 and part == HI and g == 0 and wp == HI),
                                                    stop=(c == CHUNKS - 1 and part == LO), skip_group_check=True)
                        if c == CHUNKS - 1:
                            ins.then_inc(out_done, 1)
                if at(q, "turn_adj") and nxt is not None:
                    pe.wait_ge(normed_ready, CHUNKS * m + CHUNKS)
                    turn_adj(s, nxt)

            def prepare(s, n, q):
                m = order(s, n)
                if at(q, "turn_state0"):
                    pe.wait_ge(node0_ready, m + 1)
                    if isinstance(m, int) and m <= STREAMS:
                        pe.wait_ge(adjT_ready, STREAMS)
                        if m > 0:
                            pe.wait_ge(state0_parts_ready, m)
                    else:
                        pe.wait_ge(adjT_ready, m)
                    turn(b_q, node0_parts, HI)
                    turn(b_q, node0_parts, LO).then_inc(state0_turned, 1)

            setup()
            for s in range(STREAMS):
                if s > 0:
                    pe.wait_ge(adjT_ready, s)
                turn_adj(s, 0)
            schedule(pe, layer, tail, prepare)


_INS = ["x", "adj", "nodemask", "L0_gnn_weight", "L0_gnn_w_ih", "L0_gnn_w_hh", "L0_gnn_b_ih", "L0_gnn_b_hh",
        "L1_gnn_epsilon", "L1_gnn_W1", "L1_gnn_b1", "L1_gnn_rms_weight", "L1_gnn_W2", "L1_gnn_b2"]
_OUTS = [((128, 128, 128), "float32")]


def kernel(**inputs):
    import numpy as _np
    import concourse.bacc as _bacc
    from concourse import mybir as _mybir
    from concourse.bass_utils import run_bass_kernel_spmd as _run

    nc = _bacc.Bacc("TRN2", target_bir_lowering=False, num_devices=1)
    arrays, args = {}, []
    for name in _INS:
        a = _np.ascontiguousarray(inputs[name])
        if name == "L1_gnn_epsilon":
            a = a.reshape(1)
        arrays[f"in_{name}_dram"] = a
        args.append(nc.dram_tensor(f"in_{name}_dram", a.shape, _mybir.dt.from_np(a.dtype), kind="ExternalInput").ap())
    for i, (shape, dtype) in enumerate(_OUTS):
        dt = _mybir.dt.from_np(_np.dtype(dtype))
        args.append(nc.dram_tensor(f"out_{i}_dram", shape, dt, kind="ExternalOutput").ap())
    gnn_pair_kernel(nc, *args)
    r = _run(nc, [arrays], core_ids=[0])
    got = tuple(r.results[0][f"out_{i}_dram"] for i in range(len(_OUTS)))
    return got[0]
```

```python
from contextlib import ExitStack

import concourse.bass as bass
from concourse import mybir

ALU = mybir.AluOpType
ACT = mybir.ActivationFunctionType
F32 = mybir.dt.float32
F16 = mybir.dt.float16

P = 128
HI, LO = 0, 1

STATE_SCALE = 2.0 ** 5
WEIGHT_SCALE = 2.0 ** 8
GATE_SCALE = STATE_SCALE * WEIGHT_SCALE
AGG_SCALE = 2.0 ** 3
GRAM_SCALE = 2.0 ** 6
ACTIVE_SCALE = 2.0 ** 5
LN_EPS = 1e-5
RMS_EPS = 1e-6

GRAPHS = 4
STREAMS = 2
STEP = 26

AT_LAYER = dict(
    turn_hi=0, hidden_r_hi=0, turn_lo=0, hidden_r_lo=2, agg_of_hi=4, agg_of_lo=4, hidden_n=6,
    input_r=8, input_n=11, gate_z=12,
    copy_hi=3, copy_lo=4, agg_hi=6, sigmoid_r=8, sigmoid_z=15, tanh=20, state_hi=24,
    agg_lo=0, reset=4, add_input=9, z_state=11, mix=14, new_state=14, edges=4,
    state_lo=13,
)
AT_TAIL = dict(
    back=8, sums=24, gram=27, mean_sq=32, rows=37, chunk0=34, chunk1=40, chunk2=45, chunk3=50,
    project0=58, project1=71, project2=78, project3=83, turn_adj=52, turn_state0=61,
    relu1=20, sums_hi=26, copy_rows=38, sigmoid0=43, sigmoid1=45, sigmoid2=48, sigmoid3=66,
    hi0=46, hi1=59, hi2=72, hi3=79, node_hi0=51, copy_state0=60,
    x1=1, stats1=4, spread1=4, variance1=7, shift1=11, sums_lo=17, gram_prod=22,
    mean_sq_read=26, norm0=29, norm1=36, norm2=39, norm3=44, out=80, stats0=15, spread0=15,
    variance0=17, shift0=23, norm0_in=28, node_lo0=46, add_epsilon=48,
    silu0=38, silu1=39, silu2=44, silu3=52, x1_b2=18, pow1=8, pow_ms=20, pow0=17, lo0=40,
    lo1=48, lo2=60, lo3=70, state0=53,
    load_adj=3, load_res=5, load_x=34, store=52,
)


def gnn_pair_kernel(nc, x, adj, nodemask, gru_weight, w_ih, w_hh, b_ih, b_hh,
                    epsilon, W1, b1, rms_weight, W2, b2, out):
    B, N, D = x.shape
    LAYERS = gru_weight.shape[0]
    H = W1.shape[1]
    CHUNKS = H // P
    COLS = GRAPHS * N
    ROUNDS = B // (GRAPHS * STREAMS)
    SPAN = LAYERS * STEP
    HALF = SPAN // 2
    SUM_SCALE = AGG_SCALE * GRAM_SCALE
    SQUARE_TO_ROWS = ACTIVE_SCALE * (H * SUM_SCALE) ** 0.5 / (AGG_SCALE * WEIGHT_SCALE)
    RST, UPD, NEW = 0, 1, 2
    assert N == P and D == P and COLS == 512 and ROUNDS > 3

    x_v = x.rearrange("(k g) p d -> k p g d", g=GRAPHS)
    adj_v = adj.rearrange("(k g) p d -> k p g d", g=GRAPHS)
    out_v = out.rearrange("(k g) p d -> k p g d", g=GRAPHS)

    ctx = ExitStack()
    with ctx:
        def sb(name, shape, dt):
            return ctx.enter_context(nc.sbuf_tensor(name, shape, dt))

        def sem(name):
            return ctx.enter_context(nc.semaphore(name))

        def sem_pair(name):
            return [sem(f"{name}{s}") for s in range(STREAMS)]

        def buf(name, shape, dt=F32):
            return [sb(f"{name}{s}", [P] + shape, dt) for s in range(STREAMS)]

        ident = sb("ident", [P, P], F32)
        ident16 = sb("ident16", [P, P], F16)
        ones = sb("ones", [P, P], F32)
        minus_half = sb("minus_half", [P, GRAPHS], F32)
        w_ih_in = sb("w_ih_in", [P, 3, D], F32)
        w_hh_in = sb("w_hh_in", [P, 3, D], F32)
        gru_in = sb("gru_in", [P, LAYERS, D], F32)
        w_ihT = sb("w_ihT", [P, 3 * P], F32)
        w_hhT = sb("w_hhT", [P, 3 * P], F32)
        gruT = sb("gruT", [P, LAYERS, P], F32)
        w_state = sb("w_state", [P, 2, 3 * P], F16)
        w_agg = [sb(f"w_agg{l}", [P, 2, 3 * P], F16) for l in range(LAYERS)]
        bih_in = sb("bih_in", [P, 3], F32)
        bhh_in = sb("bhh_in", [P, 3], F32)
        gate_bias = sb("gate_bias", [P, 2], F32)
        hn_bias = sb("hn_bias", [P, 1], F32)
        w1_in = sb("w1_in", [P, H], F32)
        w1T = sb("w1T", [P, CHUNKS, P], F32)
        w1 = sb("w1", [P, 2, H], F16)
        gram = sb("gram", [P, 2, P], F16)
        gram_bias = sb("gram_bias", [P, 1], F32)
        b1_in = sb("b1_in", [P, CHUNKS], F32)
        b1_scaled = sb("b1_scaled", [P, CHUNKS], F32)
        b1_squares = sb("b1_squares", [P, CHUNKS], F32)
        minus_b1_norm = sb("minus_b1_norm", [P, 1], F32)
        b1_norm_eps = sb("b1_norm_eps", [P, 1], F32)
        rms_w = sb("rms_w", [P, CHUNKS], F32)
        rms_w_rows = sb("rms_w_rows", [P, H], F32)
        w1_rms = sb("w1_rms", [P, H], F32)
        w2_in = sb("w2_in", [P, CHUNKS, D], F32)
        w2 = sb("w2", [P, 2, CHUNKS, D], F16)
        b2_rows = sb("b2_rows", [P, D], F32)
        eps_col = sb("eps_col", [P, 1], F32)
        eps_ident = sb("eps_ident", [P, P], F32)
        mask_in = sb("mask_in", [B, N], F32)
        maskT = sb("maskT", [N, B], F32)

        adj_in = buf("adj_in", [GRAPHS, N])
        edges = buf("edges", [GRAPHS, N], F16)
        adjT = buf("adjT", [GRAPHS, N])
        state = buf("state", [COLS])
        state_parts = buf("state_parts", [2, COLS], F16)
        node_parts = buf("node_parts", [2, COLS], F16)
        agg_parts = buf("agg_parts", [2, COLS], F16)
        rgate = buf("rgate", [COLS])
        zgate = buf("zgate", [COLS])
        reset_hn = buf("reset_hn", [COLS])
        npre = buf("npre", [COLS])
        ncand = buf("ncand", [COLS])
        zstate = buf("zstate", [COLS])
        nmix = buf("nmix", [COLS])
        xout = buf("xout", [GRAPHS, D])

        def one(name, shape, dt=F32):
            return sb(name, [P] + shape, dt)

        ln_in = [one("xin", [GRAPHS, D]), one("x1", [GRAPHS, D])]
        ln_out = [one(f"ln_out{k}", [GRAPHS, D]) for k in range(2)]
        ln_stats = [one(f"ln_stats{k}", [GRAPHS, 6]) for k in range(2)]
        ln_mean2 = [one(f"ln_mean2{k}", [GRAPHS]) for k in range(2)]
        ln_diff = [one(f"ln_diff{k}", [GRAPHS]) for k in range(2)]
        ln_diff2 = [one(f"ln_diffsq{k}", [GRAPHS]) for k in range(2)]
        ln_sq = [one(f"ln_sq{k}", [GRAPHS]) for k in range(2)]
        ln_var = [one(f"ln_var{k}", [GRAPHS]) for k in range(2)]
        ln_rstd = [one(f"ln_rstd{k}", [GRAPHS]) for k in range(2)]
        ln_shift = [one(f"ln_shift{k}", [GRAPHS]) for k in range(2)]
        xin, x1 = ln_in
        node0_parts = one("first_node_parts", [2, COLS], F16)
        state0_parts = one("first_state_parts", [2, COLS], F16)
        state0 = one("first_state", [COLS])
        xres = one("xres", [GRAPHS, D])
        x1_b2 = one("x1_b2", [GRAPHS, D])
        sum_parts = one("sum_parts", [2, COLS], F16)
        sums = one("sums", [COLS])
        gram_prod = one("gram_prod", [COLS])
        mean_sq = one("mean_sq", [GRAPHS])
        rms = one("rms", [GRAPHS])
        rms_rows = one("rms_rows", [COLS])
        normed = [one(f"normed{c}", [COLS]) for c in range(CHUNKS)]
        sigm = [one(f"sigm{c}", [COLS]) for c in range(CHUNKS)]
        active = [one(f"active{c}", [COLS]) for c in range(CHUNKS)]
        active_parts = [one(f"active_parts{c}", [2, COLS], F16) for c in range(CHUNKS)]

        def bank(name):
            return ctx.enter_context(nc.psum_tensor(name, [P, COLS], F32))

        b_rz = [bank(f"b_rz{s}") for s in range(STREAMS)]
        b_h = [bank(f"b_h{s}") for s in range(STREAMS)]
        b_x = [bank(f"b_x{s}") for s in range(STREAMS)]
        b_p = bank("b_p")
        b_q = bank("b_q")
        spots = [b_rz[0], b_h[0], b_x[0], b_p, b_rz[1]]

        def half_view(bank):
            return bank[:, :].bitcast(F16).rearrange("p (a c) -> p a c", a=2)

        adj_loaded, stored = sem_pair("adj_loaded"), sem_pair("stored")
        edges_ready = sem_pair("edges_ready")
        turned_hi, turned_lo = sem_pair("turned_hi"), sem_pair("turned_lo")
        node_hi, node_lo = sem_pair("node_hi"), sem_pair("node_lo")
        agg_done, agg_hi, agg_lo = sem_pair("agg_done"), sem_pair("agg_hi"), sem_pair("agg_lo")
        r_done, z_done, hn_done, in_done = (sem_pair("r_done"), sem_pair("z_done"),
                                            sem_pair("hn_done"), sem_pair("in_done"))
        r_ready, z_ready = sem_pair("r_ready"), sem_pair("z_ready")
        rhn_ready, npre_ready, n_ready = sem_pair("rhn_ready"), sem_pair("npre_ready"), sem_pair("n_ready")
        zh_ready, nmix_ready, h_ready = sem_pair("zh_ready"), sem_pair("nmix_ready"), sem_pair("h_ready")
        h_hi, h_lo = sem_pair("h_hi"), sem_pair("h_lo")
        xin_loaded, xres_loaded = sem("xin_loaded"), sem("xres_loaded")
        stats_done, mv_done, diff_done = sem_pair("stats_done"), sem_pair("mv_done"), sem_pair("diff_done")
        var_ready, rstd_ready = sem_pair("var_ready"), sem_pair("rstd_ready")
        shift_ready, norm_ready = sem_pair("shift_ready"), sem_pair("norm_ready")
        node0_hi, node0_ready = sem("node0_hi"), sem("node0_ready")
        state0_turned, state0_parts_ready, state0_ready = (sem("state0_turned"), sem("state0_parts_ready"),
                                                           sem("state0_ready"))
        adj_turned, adjT_ready = sem("adj_turned"), sem("adjT_ready")
        back_done, x1_ready, x1b2_ready = sem("back_done"), sem("x1_ready"), sem("x1b2_ready")
        sums_done, sums_hi, sums_ready, sums_lo = (sem("sums_done"), sem("sums_hi"),
                                                   sem("sums_ready"), sem("sums_lo"))
        gram_done, gprod_ready, ms_done = sem("gram_done"), sem("gprod_ready"), sem("ms_done")
        ms_ready, rms_ready = sem("ms_ready"), sem("rms_ready")
        rows_done, rows_ready = sem("rows_done"), sem("rows_ready")
        chunk_done, normed_ready, sigm_ready = sem("chunk_done"), sem("normed_ready"), sem("sigm_ready")
        active_ready, active_hi, active_lo = sem("active_ready"), sem("active_hi"), sem("active_lo")
        out_done, xout_ready = sem("out_done"), sem("xout_ready")
        params_loaded, w_loaded = sem("params_loaded"), sem("w_loaded")
        ident_zero, consts_ready = sem("ident_zero"), sem("consts_ready")
        w_turned, w_copied, w_product, setup_chain, weights_ready = (
            sem("w_turned"), sem("w_copied"), sem("w_product"), sem("setup_chain"), sem("weights_ready"))
        hi_ready = sem("hi_ready")

        def schedule(eng, layer, tail, prepare):
            def stream(s, n, t):
                layer(s, n, t // STEP, t % STEP)

            def second(s, n, t, nxt, late=True):
                if late:
                    tail(1 - s, n if s == 1 else n - 1, t + HALF, None)
                tail(s, n, t, nxt)

            def round_of(i, first=False):
                for t in range(HALF):
                    stream(0, i, t)
                    stream(1, i - 1, t + HALF)
                    second(0, i - 1, t, i, not first)
                    prepare(1, i, t)
                for t in range(HALF):
                    stream(0, i, t + HALF)
                    stream(1, i, t)
                    second(1, i - 1, t, i)
                    if not (isinstance(i, int) and i == ROUNDS - 1):
                        prepare(0, i + 1, t)

            for t in range(HALF):
                stream(0, 0, t)
                prepare(1, 0, t)
            for t in range(HALF):
                stream(0, 0, t + HALF)
                stream(1, 0, t)
                prepare(0, 1, t)
            round_of(1, first=True)
            with eng.Fori(2, ROUNDS - 1) as i:
                round_of(i)
            last = ROUNDS - 1
            round_of(last)
            for t in range(HALF):
                stream(1, last, t + HALF)
                second(0, last, t, None)
            for t in range(HALF):
                second(1, last, t, None)
            for t in range(HALF):
                tail(1, last, t + HALF, None)

        def order(s, n):
            return STREAMS * n + s

        def at(q, step):
            return q == AT_TAIL[step]

        def at_layer(q, step):
            return q == AT_LAYER[step]

        block = ctx.enter_context(nc.Block())

        @block.sync
        def _(sp):
            def load_xin(s, n):
                sp.dma_start(xin[:, :, :], x_v[STREAMS * n + 1 - s]).then_inc(xin_loaded, 16)

            def load_xres(s, n):
                sp.dma_start(xres[:, :, :], x_v[STREAMS * n + 1 - s]).then_inc(xres_loaded, 16)

            def load_adj(s, n):
                sp.dma_start(adj_in[s][:, :, :], adj_v[STREAMS * n + 1 - s]).then_inc(adj_loaded[s], 16)

            sp.dma_start(w_ih_in[:, :, :], w_ih.rearrange("(g p) e -> p g e", p=P)).then_inc(w_loaded, 16)
            sp.dma_start(gru_in[:, :, :], gru_weight.rearrange("l d e -> d l e")).then_inc(w_loaded, 16)
            sp.dma_start(w_hh_in[:, :, :], w_hh.rearrange("(g p) e -> p g e", p=P)).then_inc(w_loaded, 16)
            sp.dma_start(w1_in[:, :], W1).then_inc(w_loaded, 16)
            sp.dma_start(mask_in[:, :], nodemask).then_inc(w_loaded, 16)
            load_xin(0, 0)
            load_adj(0, 0)
            load_adj(1, 0)
            sp.dma_start(w2_in[:, :, :], W2.rearrange("(c p) d -> p c d", p=P)).then_inc(params_loaded, 16)
            with nc.allow_non_contiguous_dma(reason="bias columns of a few hundred numbers, once"):
                sp.dma_start(bih_in[:, :], b_ih.rearrange("(g p) -> p g", p=P)).then_inc(params_loaded, 16)
                sp.dma_start(bhh_in[:, :], b_hh.rearrange("(g p) -> p g", p=P)).then_inc(params_loaded, 16)
                sp.dma_start(b1_in[:, :], b1.rearrange("(c p) -> p c", p=P)).then_inc(params_loaded, 16)
                sp.dma_start(rms_w[:, :], rms_weight.rearrange("(c p) -> p c", p=P)).then_inc(params_loaded, 16)
            sp.dma_start(rms_w_rows[:, :], rms_weight.partition_broadcast(P)).then_inc(params_loaded, 16)
            sp.dma_start(b2_rows[:, :], b2.partition_broadcast(P)).then_inc(params_loaded, 16)
            sp.dma_start(eps_col[:, :], epsilon.partition_broadcast(P)).then_inc(params_loaded, 16)
            load_xres(0, 0)
            sp.wait_ge(norm_ready[0], GRAPHS)
            load_xin(1, 0)

            def layer(s, n, l, q):
                pass

            def tail(s, n, q, nxt):
                m = order(s, n)
                if at(q, "load_res") and not (s == 1 and nxt is None):
                    sp.wait_ge(x1_ready, m + 1)
                    load_xres(1 - s, n if s == 0 else nxt)
                if at(q, "store"):
                    sp.wait_ge(xout_ready, m + 2)
                    sp.dma_start(out_v[STREAMS * n + 1 - s], xout[s][:, :, :]).then_inc(stored[s], 16)

            def prepare(s, n, q):
                last_one = s == 1 and isinstance(n, int) and n == ROUNDS - 1
                if at(q, "load_x") and not last_one:
                    sp.wait_ge(norm_ready[0], GRAPHS * order(s, n) + GRAPHS)
                    load_xin(1 - s, n if s == 0 else n + 1)
                if at(q, "load_adj") and not (isinstance(n, int) and n == 0):
                    sp.wait_ge(edges_ready[s], n)
                    sp.wait_ge(adj_turned, order(s, n - 1) + 1)
                    load_adj(s, n)

            schedule(sp, layer, tail, prepare)
            for s in range(STREAMS):
                sp.wait_ge(stored[s], 16 * ROUNDS + 16)

        @block.gpsimd
        def _(pool):
            pool.memset(ident[:, :], 0.0).then_inc(ident_zero, 1)
            pool.memset(ones[:, :], 1.0)
            pool.memset(minus_half[:, :], -0.5)
            pool.wait_ge(ident_zero, 1)
            pool.affine_select(out=ident[:, :], in_=ident[:, :], compare_op=ALU.not_equal, fill=1.0, base=0,
                               pattern=[[-1, P]], channel_multiplier=1).then_inc(consts_ready, 1)
            pool.wait_ge(consts_ready, 1)

            def rstd(m, k):
                pool.wait_ge(var_ready[k], m + 1)
                pool.tensor_tensor(ln_rstd[k][:, :], ln_var[k][:, :], minus_half[:, :], ALU.pow)\
                    .then_inc(rstd_ready[k], 1)

            def join_state0(m):
                pool.wait_ge(state0_parts_ready, m + 1)
                pool.tensor_tensor(state0[:, :], state0_parts[:, HI, :], state0_parts[:, LO, :], ALU.add)\
                    .then_inc(state0_ready, 1)

            def layer(s, n, l, q):
                if at_layer(q, "state_lo"):
                    pool.wait_ge(h_hi[s], LAYERS * n + l + 1)
                    pool.tensor_tensor(state_parts[s][:, LO, :], state[s][:, :], state_parts[s][:, HI, :],
                                       ALU.subtract).then_inc(h_lo[s], 1)

            def tail(s, n, q, nxt):
                m = order(s, n)
                if at(q, "x1_b2"):
                    pool.wait_ge(xout_ready, m + 1)
                    pool.wait_ge(x1_ready, m + 1)
                    pool.tensor_tensor(x1_b2[:, :, :], x1[:, :, :],
                                       b2_rows[:, :].unsqueeze(1).to_broadcast([P, GRAPHS, D]), ALU.add)\
                        .then_inc(x1b2_ready, 1)
                if at(q, "pow1"):
                    rstd(m, 1)
                if at(q, "pow_ms"):
                    pool.wait_ge(ms_ready, m + 1)
                    pool.tensor_tensor(rms[:, :], mean_sq[:, :], minus_half[:, :], ALU.pow)\
                        .then_inc(rms_ready, 1)
                for c in range(CHUNKS):
                    if at(q, f"silu{c}"):
                        pool.wait_ge(sigm_ready, CHUNKS * m + c + 1)
                        pool.tensor_tensor(active[c][:, :], normed[c][:, :], sigm[c][:, :], ALU.mult)\
                            .then_inc(active_ready, 1)
                    if at(q, f"lo{c}"):
                        pool.wait_ge(active_hi, CHUNKS * m + c + 1)
                        pool.tensor_tensor(active_parts[c][:, LO, :], active[c][:, :],
                                           active_parts[c][:, HI, :], ALU.subtract).then_inc(active_lo, 1)

            def prepare(s, n, q):
                if at(q, "pow0"):
                    rstd(order(s, n), 0)
                if at(q, "state0"):
                    join_state0(order(s, n))

            rstd(0, 0)
            join_state0(0)
            schedule(pool, layer, tail, prepare)

        @block.scalar
        def _(act):
            act.preload_act_table_set("sigmoid_and_others")

            def setup():
                act.wait_ge(w_turned, 1)
                act.activation(w_state[:, HI, :], b_rz[1][:, 0:3 * P], ACT.Copy, scale=WEIGHT_SCALE)\
                    .then_inc(hi_ready, 1)
                act.activation(w1T[:, :, :], b_p[:, :].rearrange("p (c d) -> p c d", c=CHUNKS), ACT.Copy)
                act.activation(maskT[:, :], b_h[1][:, 0:B], ACT.Copy, scale=1.0 / STATE_SCALE).then_inc(w_copied, 1)
                node_hi0(0)
                for l in range(LAYERS):
                    act.wait_ge(w_product, l + 1)
                    act.activation(w_agg[l][:, HI, :], spots[l][:, 0:3 * P], ACT.Copy, scale=WEIGHT_SCALE)\
                        .then_inc(hi_ready, 1)
                copy_state0(0)

            def node_hi0(m):
                act.wait_ge(norm_ready[0], GRAPHS * m + GRAPHS)
                act.activation(node0_parts[:, HI, :].rearrange("p (g d) -> p g d", g=GRAPHS),
                               ln_out[0][:, :, :], ACT.Relu).then_inc(node0_hi, 1)

            def copy_state0(m):
                act.wait_ge(state0_turned, m + 1)
                act.activation(state0_parts[:, :, :], half_view(b_q), ACT.Copy).then_inc(state0_parts_ready, 1)

            def layer(s, n, l, q):
                k = LAYERS * n + l + 1
                if at_layer(q, "copy_hi") and l > 0:
                    act.wait_ge(turned_hi[s], (LAYERS - 1) * n + l)
                    act.activation(node_parts[s][:, HI, :], half_view(b_x[s])[:, HI, :], ACT.Copy)\
                        .then_inc(node_hi[s], 1)
                if at_layer(q, "copy_lo") and l > 0:
                    act.wait_ge(turned_lo[s], (LAYERS - 1) * n + l)
                    act.activation(node_parts[s][:, LO, :], half_view(b_h[s])[:, LO, :], ACT.Copy)\
                        .then_inc(node_lo[s], 1)
                if at_layer(q, "agg_hi"):
                    act.wait_ge(agg_done[s], k)
                    act.activation(agg_parts[s][:, HI, :], b_x[s][:, :], ACT.Copy).then_inc(agg_hi[s], 1)
                if at_layer(q, "sigmoid_r"):
                    act.wait_ge(r_done[s], k)
                    act.activation(rgate[s][:, :], b_rz[s][:, :], ACT.Sigmoid, bias=gate_bias[:, RST:RST + 1],
                                   scale=1.0 / GATE_SCALE).then_inc(r_ready[s], 1)
                if at_layer(q, "sigmoid_z"):
                    act.wait_ge(z_done[s], k)
                    act.activation(zgate[s][:, :], b_rz[s][:, :], ACT.Sigmoid, bias=gate_bias[:, UPD:UPD + 1],
                                   scale=1.0 / GATE_SCALE).then_inc(z_ready[s], 1)
                if at_layer(q, "tanh"):
                    act.wait_ge(npre_ready[s], k)
                    act.activation(ncand[s][:, :], npre[s][:, :], ACT.Tanh, bias=bih_in[:, NEW:NEW + 1],
                                   scale=1.0 / GATE_SCALE).then_inc(n_ready[s], 1)
                if at_layer(q, "state_hi"):
                    if l == 0 and not (isinstance(n, int) and n == 0):
                        act.wait_ge(back_done, order(s, n - 1) + 1)
                    act.wait_ge(h_ready[s], k)
                    act.activation(state_parts[s][:, HI, :], state[s][:, :], ACT.Copy).then_inc(h_hi[s], 1)

            def tail(s, n, q, nxt):
                m = order(s, n)
                if at(q, "relu1"):
                    act.wait_ge(shift_ready[1], m + 1)
                    for g in range(GRAPHS):
                        act.activation(ln_out[1][:, g, :], x1[:, g, :], ACT.Relu, bias=ln_shift[1][:, g:g + 1],
                                       scale=ln_rstd[1][:, g:g + 1]).then_inc(norm_ready[1], 1)
                if at(q, "sums_hi"):
                    act.wait_ge(sums_done, m + 1)
                    act.activation(sum_parts[:, HI, :], b_q[:, :], ACT.Copy, scale=AGG_SCALE).then_inc(sums_hi, 1)
                    act.activation(sums[:, :], b_q[:, :], ACT.Copy).then_inc(sums_ready, 1)
                if at(q, "copy_rows"):
                    act.wait_ge(rows_done, m + 1)
                    act.activation(rms_rows[:, :], b_p[:, :], ACT.Copy, scale=SQUARE_TO_ROWS).then_inc(rows_ready, 1)
                for c in range(CHUNKS):
                    if at(q, f"sigmoid{c}"):
                        act.wait_ge(normed_ready, CHUNKS * m + c + 1)
                        act.activation(sigm[c][:, :], normed[c][:, :], ACT.Sigmoid, scale=1.0 / ACTIVE_SCALE)\
                            .then_inc(sigm_ready, 1)
                    if at(q, f"hi{c}"):
                        act.wait_ge(active_ready, CHUNKS * m + c + 1)
                        act.activation(active_parts[c][:, HI, :], active[c][:, :], ACT.Copy).then_inc(active_hi, 1)

            def prepare(s, n, q):
                m = order(s, n)
                if at(q, "node_hi0"):
                    node_hi0(m)
                if at(q, "copy_state0"):
                    copy_state0(m)

            setup()
            schedule(act, layer, tail, prepare)

        @block.vector
        def _(dve):
            chain = [0]

            def link(ins):
                chain[0] += 1
                ins.then_inc(setup_chain, 1)
                dve.wait_ge(setup_chain, chain[0])

            def low(dst_lo, src, scale, dst_hi):
                return dve.scalar_tensor_tensor(out=dst_lo, in0=src, scalar=scale, in1=dst_hi,
                                                op0=ALU.mult, op1=ALU.subtract)

            def split(dst_hi, dst_lo, src, scale):
                link(dve.tensor_scalar(dst_hi, src, scale, None, ALU.mult))
                return low(dst_lo, src, scale, dst_hi)

            def setup():
                dve.wait_ge(consts_ready, 1)
                dve.tensor_copy(ident16[:, :], ident[:, :])
                statistics(0, 0)
                spread(0, 0)
                variance(0, 0)
                take_edges(0, 0)
                dve.wait_ge(w_turned, 1)
                dve.tensor_copy(w_ihT[:, :], b_rz[0][:, 0:3 * P])
                dve.tensor_copy(gruT[:, 0:4, :], b_h[0][:, :].rearrange("p (l d) -> p l d", l=4))
                dve.tensor_copy(gruT[:, 4, :], b_x[0][:, 0:P]).then_inc(w_copied, 1)
                dve.wait_ge(hi_ready, 1)
                low(w_state[:, LO, :], b_rz[1][:, 0:3 * P], WEIGHT_SCALE, w_state[:, HI, :]).then_inc(w_copied, 1)
                shift(0, 0)
                normalize0(0)
                node_lo0(0)
                dve.wait_ge(params_loaded, 16 * 8)
                dve.tensor_tensor(gate_bias[:, :], bih_in[:, 0:2], bhh_in[:, 0:2], ALU.add).then_inc(stored[0], 16)
                dve.tensor_scalar(hn_bias[:, :], bhh_in[:, NEW:NEW + 1], GATE_SCALE, None, ALU.mult)\
                    .then_inc(stored[1], 16)
                dve.scalar_tensor_tensor(out=b1_scaled[:, :], in0=b1_in[:, :], scalar=AGG_SCALE * WEIGHT_SCALE,
                                         in1=rms_w[:, :], op0=ALU.mult, op1=ALU.mult).then_inc(xout_ready, 1)
                link(dve.tensor_scalar(eps_ident[:, :], ident[:, :], eps_col[:, 0:1], None, ALU.mult))
                add_epsilon(0, 0, b_q)
                add_epsilon(1, 1, b_x[1])
                dve.tensor_tensor(b1_squares[:, :], b1_in[:, :], b1_in[:, :], ALU.mult).then_inc(w_copied, 1)
                for l in range(LAYERS):
                    dve.wait_ge(hi_ready, l + 2)
                    low(w_agg[l][:, LO, :], spots[l][:, 0:3 * P], WEIGHT_SCALE, w_agg[l][:, HI, :])\
                        .then_inc(weights_ready, 1)
                dve.wait_ge(w_product, LAYERS + 1)
                split(gram[:, HI, :], gram[:, LO, :], b_h[1][:, 0:P], GRAM_SCALE)
                dve.tensor_scalar(gram_bias[:, :], b_x[1][:, 0:1], 2.0 * GRAM_SCALE * AGG_SCALE, None, ALU.mult)
                dve.tensor_scalar(minus_b1_norm[:, :], b_x[1][:, 1:2], -SUM_SCALE, None, ALU.mult)
                dve.tensor_scalar(b1_norm_eps[:, :], b_x[1][:, 1:2], SUM_SCALE, H * RMS_EPS * SUM_SCALE,
                                  ALU.mult, ALU.add).then_inc(weights_ready, 1)
                take_edges(1, 0)
                link(dve.tensor_tensor(w1_rms[:, :], w1_in[:, :], rms_w_rows[:, :], ALU.mult))
                split(w1[:, HI, :], w1[:, LO, :], w1_rms[:, :], WEIGHT_SCALE)
                split(w2[:, HI, :, :], w2[:, LO, :, :], w2_in[:, :, :], WEIGHT_SCALE)

            def statistics(m, k):
                if k == 0:
                    dve.wait_ge(xin_loaded, 16 * m + 16)
                else:
                    dve.wait_ge(x1_ready, m + 1)
                for g in range(GRAPHS):
                    ins = dve.bn_stats(ln_stats[k][:, g, :], ln_in[k][:, g, :])
                ins.then_inc(stats_done[k], 1)

            def spread(m, k):
                dve.wait_ge(stats_done[k], m + 1)
                st = ln_stats[k]
                dve.tensor_tensor(ln_diff[k][:, :], st[:, :, 1], st[:, :, 4], ALU.subtract).then_inc(mv_done[k], 1)
                dve.tensor_tensor(ln_mean2[k][:, :], st[:, :, 1], st[:, :, 4], ALU.add)
                dve.scalar_tensor_tensor(out=ln_sq[k][:, :], in0=st[:, :, 2], scalar=LN_EPS * D,
                                         in1=st[:, :, 5], op0=ALU.add, op1=ALU.add)

            def variance(m, k):
                scale = STATE_SCALE ** -2 if k == 0 else 1.0
                dve.wait_ge(mv_done[k], m + 1)
                dve.scalar_tensor_tensor(out=ln_diff2[k][:, :], in0=ln_diff[k][:, :], scalar=0.25 * scale,
                                         in1=ln_diff[k][:, :], op0=ALU.mult, op1=ALU.mult).then_inc(diff_done[k], 1)
                dve.wait_ge(diff_done[k], m + 1)
                dve.scalar_tensor_tensor(out=ln_var[k][:, :], in0=ln_sq[k][:, :], scalar=scale / D,
                                         in1=ln_diff2[k][:, :], op0=ALU.mult, op1=ALU.add)\
                    .then_inc(var_ready[k], 1)

            def shift(m, k):
                dve.wait_ge(rstd_ready[k], m + 1)
                dve.scalar_tensor_tensor(out=ln_shift[k][:, :], in0=ln_mean2[k][:, :], scalar=-0.5,
                                         in1=ln_rstd[k][:, :], op0=ALU.mult, op1=ALU.mult)\
                    .then_inc(shift_ready[k], 1)

            def normalize0(m):
                dve.wait_ge(shift_ready[0], m + 1)
                for g in range(GRAPHS):
                    dve.tensor_scalar(ln_out[0][:, g, :], xin[:, g, :], ln_rstd[0][:, g:g + 1],
                                      ln_shift[0][:, g:g + 1], ALU.mult, ALU.add).then_inc(norm_ready[0], 1)

            def node_lo0(m):
                dve.wait_ge(node0_hi, m + 1)
                dve.scalar_tensor_tensor(out=node0_parts[:, LO, :].rearrange("p (g d) -> p g d", g=GRAPHS),
                                         in0=ln_out[0][:, :, :], scalar=0.0,
                                         in1=node0_parts[:, HI, :].rearrange("p (g d) -> p g d", g=GRAPHS),
                                         op0=ALU.max, op1=ALU.subtract).then_inc(node0_ready, 1)

            def take_edges(s, n):
                dve.wait_ge(adj_loaded[s], 16 * n + 16)
                dve.tensor_scalar(edges[s][:, :, :], adj_in[s][:, :, :], 0.0, None, ALU.not_equal)\
                    .then_inc(edges_ready[s], 1)

            def add_epsilon(s, m, bank):
                dve.wait_ge(adj_turned, m + 1)
                dve.tensor_tensor(adjT[s][:, :, :], bank[:, :].rearrange("p (g d) -> p g d", g=GRAPHS),
                                  eps_ident[:, :].unsqueeze(1).to_broadcast([P, GRAPHS, N]), ALU.add)\
                    .then_inc(adjT_ready, 1)

            def layer(s, n, l, q):
                k = LAYERS * n + l + 1
                if at_layer(q, "agg_lo"):
                    dve.wait_ge(agg_hi[s], k)
                    dve.tensor_tensor(agg_parts[s][:, LO, :], b_x[s][:, :], agg_parts[s][:, HI, :], ALU.subtract)\
                        .then_inc(agg_lo[s], 1)
                if at_layer(q, "reset"):
                    dve.wait_ge(r_ready[s], k)
                    dve.wait_ge(hn_done[s], k)
                    dve.scalar_tensor_tensor(out=reset_hn[s][:, :], in0=b_h[s][:, :], scalar=hn_bias[:, 0:1],
                                             in1=rgate[s][:, :], op0=ALU.add, op1=ALU.mult)\
                        .then_inc(rhn_ready[s], 1)
                if at_layer(q, "add_input"):
                    dve.wait_ge(rhn_ready[s], k)
                    dve.wait_ge(in_done[s], k)
                    dve.tensor_tensor(npre[s][:, :], b_x[s][:, :], reset_hn[s][:, :], ALU.add)\
                        .then_inc(npre_ready[s], 1)
                if at_layer(q, "z_state"):
                    dve.wait_ge(z_ready[s], k)
                    if l == 0:
                        dve.wait_ge(state0_ready, order(s, n) + 1)
                    old = state0 if l == 0 else state[s]
                    dve.tensor_tensor(zstate[s][:, :], zgate[s][:, :], old[:, :], ALU.mult)\
                        .then_inc(zh_ready[s], 1)
                if at_layer(q, "mix"):
                    dve.wait_ge(n_ready[s], k)
                    dve.wait_ge(z_ready[s], k)
                    dve.scalar_tensor_tensor(out=nmix[s][:, :], in0=zgate[s][:, :], scalar=-1.0, in1=ncand[s][:, :],
                                             op0=ALU.add, op1=ALU.mult).then_inc(nmix_ready[s], 1)
                if at_layer(q, "new_state"):
                    dve.wait_ge(nmix_ready[s], k)
                    dve.wait_ge(zh_ready[s], k)
                    dve.scalar_tensor_tensor(out=state[s][:, :], in0=nmix[s][:, :], scalar=-STATE_SCALE,
                                             in1=zstate[s][:, :], op0=ALU.mult, op1=ALU.add)\
                        .then_inc(h_ready[s], 1)
                if at_layer(q, "edges") and l == LAYERS - 1 and not (isinstance(n, int) and n == ROUNDS - 1):
                    dve.wait_ge(agg_done[s], k)
                    take_edges(s, n + 1)

            def tail(s, n, q, nxt):
                m = order(s, n)
                if at(q, "x1"):
                    dve.wait_ge(back_done, m + 1)
                    dve.wait_ge(xres_loaded, 16 * m + 16)
                    first = (n * STREAMS + 1 - s) * GRAPHS
                    for g in range(GRAPHS):
                        ins = dve.scalar_tensor_tensor(out=x1[:, g, :], in0=b_q[:, g * P:(g + 1) * P],
                                                       scalar=maskT[:, bass.ds(first + g, 1)], in1=xres[:, g, :],
                                                       op0=ALU.mult, op1=ALU.add)
                    ins.then_inc(x1_ready, 1)
                if at(q, "stats1"):
                    statistics(m, 1)
                if at(q, "spread1"):
                    spread(m, 1)
                if at(q, "variance1"):
                    variance(m, 1)
                if at(q, "shift1"):
                    shift(m, 1)
                if at(q, "sums_lo"):
                    dve.wait_ge(sums_hi, m + 1)
                    dve.wait_ge(sums_ready, m + 1)
                    dve.scalar_tensor_tensor(out=sum_parts[:, LO, :], in0=b_q[:, :], scalar=AGG_SCALE,
                                             in1=sum_parts[:, HI, :], op0=ALU.mult, op1=ALU.subtract)\
                        .then_inc(sums_lo, 1)
                if at(q, "gram_prod"):
                    dve.wait_ge(gram_done, m + 1)
                    dve.scalar_tensor_tensor(out=gram_prod[:, :], in0=b_p[:, :], scalar=gram_bias[:, 0:1],
                                             in1=sums[:, :], op0=ALU.add, op1=ALU.mult).then_inc(gprod_ready, 1)
                if at(q, "mean_sq_read"):
                    dve.wait_ge(ms_done, m + 1)
                    dve.tensor_scalar(mean_sq[:, :], b_q[:, 0:GRAPHS], minus_b1_norm[:, 0:1], b1_norm_eps[:, 0:1],
                                      ALU.max, ALU.add).then_inc(ms_ready, 1)
                for c in range(CHUNKS):
                    if at(q, f"norm{c}"):
                        if c == 0:
                            dve.wait_ge(rows_ready, m + 1)
                        dve.wait_ge(chunk_done, CHUNKS * m + c + 1)
                        dve.scalar_tensor_tensor(out=normed[c][:, :], in0=b_q[:, :], scalar=b1_scaled[:, c:c + 1],
                                                 in1=rms_rows[:, :], op0=ALU.add, op1=ALU.mult)\
                            .then_inc(normed_ready, 1)
                if at(q, "add_epsilon") and nxt is not None:
                    add_epsilon(s, order(s, nxt), b_q)
                if at(q, "out"):
                    dve.wait_ge(stored[s], 16 * n + 16)
                    dve.wait_ge(x1b2_ready, m + 1)
                    dve.wait_ge(out_done, m + 1)
                    dve.scalar_tensor_tensor(out=xout[s][:, :, :],
                                             in0=b_p[:, :].rearrange("p (g d) -> p g d", g=GRAPHS),
                                             scalar=1.0 / (ACTIVE_SCALE * WEIGHT_SCALE), in1=x1_b2[:, :, :],
                                             op0=ALU.mult, op1=ALU.add).then_inc(xout_ready, 1)

            def prepare(s, n, q):
                m = order(s, n)
                if at(q, "stats0"):
                    statistics(m, 0)
                if at(q, "spread0"):
                    spread(m, 0)
                if at(q, "variance0"):
                    variance(m, 0)
                if at(q, "shift0"):
                    shift(m, 0)
                if at(q, "norm0_in"):
                    normalize0(m)
                if at(q, "node_lo0"):
                    node_lo0(m)

            setup()
            schedule(dve, layer, tail, prepare)

        @block.tensor
        def _(pe):
            def setup():
                pe.wait_ge(consts_ready, 1)
                pe.wait_ge(w_loaded, 16 * 5)
                for g in range(3):
                    pe.transpose(b_rz[0][:, g * P:(g + 1) * P], w_ih_in[:, g, :], ident[:, :])
                for l in range(LAYERS):
                    pe.transpose((b_h[0], b_x[0])[l // 4][:, (l % 4) * P:(l % 4 + 1) * P], gru_in[:, l, :],
                                 ident[:, :])
                for g in range(3):
                    pe.transpose(b_rz[1][:, g * P:(g + 1) * P], w_hh_in[:, g, :], ident[:, :])
                for c in range(CHUNKS):
                    pe.transpose(b_p[:, c * P:(c + 1) * P], w1_in[:, c * P:(c + 1) * P], ident[:, :])
                pe.transpose(b_h[1][:, 0:B], mask_in[:, :], ident[:, :]).then_inc(w_turned, 1)
                turn_adj(0, 0, b_q)
                turn_adj(1, 0, b_x[1])
                pe.wait_ge(w_copied, 3)
                for l in range(LAYERS):
                    pe.matmul(spots[l][:, 0:3 * P], gruT[:, l, :], w_ihT[:, :], start=True, stop=True)\
                        .then_inc(w_product, 1)
                turn_state0(0)
                pe.wait_ge(w_copied, 4)
                for c in range(CHUNKS):
                    pe.matmul(b_h[1][:, 0:P], w1T[:, c, :], w1T[:, c, :], start=(c == 0), stop=(c == CHUNKS - 1))
                for c in range(CHUNKS):
                    pe.matmul(b_x[1][:, 0:1], w1T[:, c, :], b1_in[:, c:c + 1],
                              start=(c == 0), stop=(c == CHUNKS - 1))
                for c in range(CHUNKS):
                    ins = pe.matmul(b_x[1][:, 1:2], ones[:, :], b1_squares[:, c:c + 1],
                                    start=(c == 0), stop=(c == CHUNKS - 1))
                ins.then_inc(w_product, 1)
                pe.wait_ge(weights_ready, LAYERS)

            def turn_adj(s, n, bank):
                pe.wait_ge(adj_loaded[s], 16 * n + 16)
                for g in range(GRAPHS):
                    ins = pe.transpose(bank[:, g * P:(g + 1) * P], adj_in[s][:, g, :], ident[:, :])
                ins.then_inc(adj_turned, 1)

            def turn_state0(m):
                pe.wait_ge(node0_ready, m + 1)
                if isinstance(m, int) and m <= STREAMS:
                    pe.wait_ge(adjT_ready, STREAMS)
                    if m > 0:
                        pe.wait_ge(state0_parts_ready, m)
                else:
                    pe.wait_ge(adjT_ready, m)
                turn(b_q, node0_parts, HI)
                turn(b_q, node0_parts, LO).then_inc(state0_turned, 1)

            def gate(out, w, g, parts, which, first, last):
                for k, (wp, ap) in enumerate(which):
                    ins = pe.matmul(out[:, :], w[:, wp, g * P:(g + 1) * P], parts[:, ap, :],
                                    start=(first and k == 0), stop=(last and k == len(which) - 1))
                return ins

            OF_HI = ((HI, HI), (LO, HI))
            OF_LO = ((HI, LO),)
            ALL = OF_HI + OF_LO

            def turn(bank, parts, part):
                for g in range(GRAPHS):
                    ins = pe.transpose(half_view(bank)[:, part, g * P:(g + 1) * P],
                                       parts[:, part, g * P:(g + 1) * P], ident16[:, :])
                return ins

            def aggregate(bank, nodes, part, graph_edges):
                for g in range(GRAPHS):
                    ins = pe.matmul(bank[:, g * P:(g + 1) * P], nodes[:, part, g * P:(g + 1) * P],
                                    graph_edges[:, g, :], start=(part == HI and g == 0), stop=(part == LO),
                                    skip_group_check=True)
                return ins

            def layer(s, n, l, q):
                k = LAYERS * n + l + 1
                old = state0_parts if l == 0 else state_parts[s]
                nodes = node0_parts if l == 0 else node_parts[s]
                if at_layer(q, "turn_hi") and l > 0:
                    pe.wait_ge(h_hi[s], k - 1)
                    turn(b_x[s], state_parts[s], HI).then_inc(turned_hi[s], 1)
                if at_layer(q, "hidden_r_hi"):
                    if l == 0:
                        pe.wait_ge(state0_parts_ready, order(s, n) + 1)
                    gate(b_rz[s], w_state, RST, old, OF_HI, True, False)
                if at_layer(q, "turn_lo") and l > 0:
                    pe.wait_ge(h_lo[s], k - 1)
                    turn(b_h[s], state_parts[s], LO).then_inc(turned_lo[s], 1)
                if at_layer(q, "hidden_r_lo"):
                    gate(b_rz[s], w_state, RST, old, OF_LO, False, False)
                if at_layer(q, "agg_of_hi"):
                    if l == 0:
                        pe.wait_ge(edges_ready[s], n + 1)
                    else:
                        pe.wait_ge(node_hi[s], (LAYERS - 1) * n + l)
                    aggregate(b_x[s], nodes, HI, edges[s])
                if at_layer(q, "agg_of_lo"):
                    if l > 0:
                        pe.wait_ge(node_lo[s], (LAYERS - 1) * n + l)
                    aggregate(b_x[s], nodes, LO, edges[s]).then_inc(agg_done[s], 1)
                if at_layer(q, "hidden_n"):
                    gate(b_h[s], w_state, NEW, old, ALL, True, True).then_inc(hn_done[s], 1)
                if at_layer(q, "input_r"):
                    pe.wait_ge(agg_hi[s], k)
                    gate(b_rz[s], w_agg[l], RST, agg_parts[s], OF_HI, False, False)
                    pe.wait_ge(agg_lo[s], k)
                    gate(b_rz[s], w_agg[l], RST, agg_parts[s], OF_LO, False, True).then_inc(r_done[s], 1)
                if at_layer(q, "input_n"):
                    gate(b_x[s], w_agg[l], NEW, agg_parts[s], ALL, True, True).then_inc(in_done[s], 1)
                if at_layer(q, "gate_z"):
                    pe.wait_ge(r_ready[s], k)
                    gate(b_rz[s], w_state, UPD, old, ALL, True, False)
                    gate(b_rz[s], w_agg[l], UPD, agg_parts[s], ALL, False, True).then_inc(z_done[s], 1)

            def tail(s, n, q, nxt):
                m = order(s, n)
                if at(q, "back"):
                    if nxt is not None:
                        pe.wait_ge(state0_parts_ready, m + 3)
                    else:
                        pe.wait_ge(adjT_ready, STREAMS * ROUNDS)
                        pe.wait_ge(normed_ready, CHUNKS * m)
                    pe.wait_ge(h_hi[s], LAYERS * n + LAYERS)
                    pe.wait_ge(h_lo[s], LAYERS * n + LAYERS)
                    for g in range(GRAPHS):
                        for part in (HI, LO):
                            ins = pe.matmul(b_q[:, g * P:(g + 1) * P], state_parts[s][:, part, g * P:(g + 1) * P],
                                            ident16[:, :], start=(part == HI), stop=(part == LO))
                    ins.then_inc(back_done, 1)
                if at(q, "sums"):
                    pe.wait_ge(adjT_ready, m + 1)
                    for g in range(GRAPHS):
                        pe.wait_ge(norm_ready[1], GRAPHS * m + g + 1)
                        ins = pe.matmul(b_q[:, g * P:(g + 1) * P], ln_out[1][:, g, :], adjT[s][:, g, :],
                                        start=True, stop=True)
                    ins.then_inc(sums_done, 1)
                if at(q, "gram"):
                    pe.wait_ge(xout_ready, m + 1)
                    pe.wait_ge(sums_hi, m + 1)
                    for part in (HI, LO):
                        pe.matmul(b_p[:, :], gram[:, part, :], sum_parts[:, HI, :], start=(part == HI), stop=False)
                    pe.wait_ge(sums_lo, m + 1)
                    pe.matmul(b_p[:, :], gram[:, HI, :], sum_parts[:, LO, :], start=False, stop=True)\
                        .then_inc(gram_done, 1)
                if at(q, "mean_sq"):
                    pe.wait_ge(gprod_ready, m + 1)
                    for g in range(GRAPHS):
                        ins = pe.matmul(b_q[:, g:g + 1], gram_prod[:, g * P:(g + 1) * P], ones[:, 0:1],
                                        start=True, stop=True)
                    ins.then_inc(ms_done, 1)
                if at(q, "rows"):
                    pe.wait_ge(rms_ready, m + 1)
                    for g in range(GRAPHS):
                        ins = pe.transpose(b_p[:, g * P:(g + 1) * P], rms[:, g:g + 1].to_broadcast([P, P]),
                                           ident[:, :])
                    ins.then_inc(rows_done, 1)
                for c in range(CHUNKS):
                    if at(q, f"chunk{c}"):
                        if c == 0:
                            pe.wait_ge(ms_ready, m + 1)
                        else:
                            pe.wait_ge(normed_ready, CHUNKS * m + c)
                        gate(b_q, w1, c, sum_parts, ALL, True, True).then_inc(chunk_done, 1)
                    if at(q, f"project{c}"):
                        if c == 0:
                            pe.wait_ge(rows_ready, m + 1)
                        for part, ready in ((HI, active_hi), (LO, active_lo)):
                            pe.wait_ge(ready, CHUNKS * m + c + 1)
                            for g in range(GRAPHS):
                                for wp in ((HI, LO) if part == HI else (HI,)):
                                    ins = pe.matmul(b_p[:, g * P:(g + 1) * P],
                                                    active_parts[c][:, part, g * P:(g + 1) * P], w2[:, wp, c, :],
                                                    start=(c == 0 and part == HI and g == 0 and wp == HI),
                                                    stop=(c == CHUNKS - 1 and part == LO), skip_group_check=True)
                        if c == CHUNKS - 1:
                            ins.then_inc(out_done, 1)
                if at(q, "turn_adj") and nxt is not None:
                    pe.wait_ge(normed_ready, CHUNKS * m + CHUNKS)
                    turn_adj(s, nxt, b_q)

            def prepare(s, n, q):
                m = order(s, n)
                if at(q, "turn_state0"):
                    turn_state0(m)

            setup()
            schedule(pe, layer, tail, prepare)


_INS = ["x", "adj", "nodemask", "L0_gnn_weight", "L0_gnn_w_ih", "L0_gnn_w_hh", "L0_gnn_b_ih", "L0_gnn_b_hh",
        "L1_gnn_epsilon", "L1_gnn_W1", "L1_gnn_b1", "L1_gnn_rms_weight", "L1_gnn_W2", "L1_gnn_b2"]
_OUTS = [((128, 128, 128), "float32")]


def kernel(**inputs):
    import numpy as _np
    import concourse.bacc as _bacc
    from concourse import mybir as _mybir
    from concourse.bass_utils import run_bass_kernel_spmd as _run

    nc = _bacc.Bacc("TRN2", target_bir_lowering=False, num_devices=1)
    arrays, args = {}, []
    for name in _INS:
        a = _np.ascontiguousarray(inputs[name])
        if name == "L1_gnn_epsilon":
            a = a.reshape(1)
        arrays[f"in_{name}_dram"] = a
        args.append(nc.dram_tensor(f"in_{name}_dram", a.shape, _mybir.dt.from_np(a.dtype), kind="ExternalInput").ap())
    for i, (shape, dtype) in enumerate(_OUTS):
        dt = _mybir.dt.from_np(_np.dtype(dtype))
        args.append(nc.dram_tensor(f"out_{i}_dram", shape, dt, kind="ExternalOutput").ap())
    gnn_pair_kernel(nc, *args)
    r = _run(nc, [arrays], core_ids=[0])
    got = tuple(r.results[0][f"out_{i}_dram"] for i in range(len(_OUTS)))
    return got[0]
```
